# Optimizing a Trainium2 kernel written in Bass

```python
import numpy as np
import jax
import jax.numpy as jnp

def _softmax(x, axis=-1):
    return jax.nn.softmax(x, axis=axis)

def _gelu(x):
    return jax.nn.gelu(x, approximate=True)

def _silu(x):
    return jax.nn.silu(x)

def _sigmoid(x):
    return jax.nn.sigmoid(x)

def _layernorm(x, axis=-1, eps=1e-05):
    m = jnp.mean(x, axis=axis, keepdims=True)
    v = jnp.var(x, axis=axis, keepdims=True)
    return (x - m) / jnp.sqrt(v + eps)

def _scatter_add(tgt, idx, src, axis=0):
    return tgt.at[idx].add(src)

def _segment_sum(src, seg, n):
    return jax.ops.segment_sum(src, seg, n)
kernel_name = 'mk_flamingo_gated_d2_seqx_r8_f4e8b2'

def setup_inputs(seed: int=0):
    np.random.seed(seed)
    _w = jnp.asarray

    def _rec_inputs():
        import jax
        import jax.numpy as jnp
        _rk = jax.random.key(seed)
        x = -7.109e-05 + 0.9999 * jax.random.normal(jax.random.fold_in(_rk, 1), (4, 256, 256), jnp.float32)
        _lenS = 256 - jax.random.randint(jax.random.fold_in(_rk, 7), (4,), 0, max(1, 256 // 4) + 1, jnp.int32)
        _lenS2 = 256 - jax.random.randint(jax.random.fold_in(_rk, 8), (4,), 0, max(1, 256 // 4) + 1, jnp.int32)
        _ctx_2048P = jax.random.normal(jax.random.fold_in(_rk, 11), (4, 16, 256), jnp.float32)
        _ctx_2048c = jax.random.dirichlet(jax.random.fold_in(_rk, 511), 0.3 * jnp.ones((16,), jnp.float32), (4, 256))
        _ctx_2048t = jnp.einsum('bsk,bkd->bsd', _ctx_2048c, _ctx_2048P)
        _ctx_2048t = _ctx_2048t * jax.lax.rsqrt(jnp.mean(jnp.square(_ctx_2048t)) + 1e-12) * 0.953939
        ctx_2048 = -3.05549e-07 + 0.0199987 * (_ctx_2048t + 0.3 * jax.random.normal(jax.random.fold_in(_rk, 611), (4, 256, 256), jnp.float32))
        _validS = jnp.arange(256)[None, :] < _lenS[:, None]
        _validS2 = jnp.arange(256)[None, :] < _lenS2[:, None]
        _causal = jnp.tril(jnp.ones((256, 256), dtype=bool))
        mask_BxS2_bk0 = jnp.logical_not(jnp.broadcast_to(_validS2[:, :], (4, 256)))
        _g = jax.random.normal(jax.random.fold_in(_rk, 9001), (2, 2), jnp.float32)
        _g = jnp.sign(_g) * jnp.maximum(jnp.abs(_g), 1.0) + (_g == 0) * 1.0
        g_xattn = _g[0]
        g_ffn = _g[1]
        return (x, ctx_2048, mask_BxS2_bk0, g_xattn, g_ffn)
    x, ctx_2048, mask_BxS2_bk0, g_xattn, g_ffn = _rec_inputs()

    def _L0_xattn_setup():
        import jax, jax.numpy as jnp
        import numpy as np
        FP8_MAX = 448.0
        ACT_EPS = 0.0001
        W_EPS = 1e-06
        BLK = 128

        def quant_dequant_act_1x128(x):
            E, M, K = x.shape
            xb = x.reshape(E, M, K // BLK, BLK)
            amax = jnp.max(jnp.abs(xb), axis=-1, keepdims=True)
            safe = jnp.maximum(amax, ACT_EPS)
            q = (xb * (FP8_MAX / safe)).astype(jnp.float8_e4m3fn)
            return (q.astype(jnp.float32) * (safe / FP8_MAX)).reshape(E, M, K)

        def quant_dequant_weight_128x128(w):
            E, N, K = w.shape
            wb = w.reshape(E, N // BLK, BLK, K // BLK, BLK)
            amax = jnp.max(jnp.abs(wb), axis=(2, 4), keepdims=True)
            safe = jnp.maximum(amax, W_EPS)
            q = (wb * (FP8_MAX / safe)).astype(jnp.float8_e4m3fn)
            return (q.astype(jnp.float32) * (safe / FP8_MAX)).reshape(E, N, K)
        key = jax.random.key(seed)
        kx, kw = jax.random.split(key)
        E, M, K, N = (8, 512, 256, 256)
        x = jax.random.normal(kx, (E, M, K), dtype=jnp.float32)
        weight = jax.random.normal(kw, (E, N, K), dtype=jnp.float32) * 0.02
        return {'x': x, 'weight': weight}
    _L0_xattn_all = _L0_xattn_setup()
    _L0_xattn_in = {k: v for k, v in _L0_xattn_all.items() if k in ()}
    del _L0_xattn_all

    def _L0_ffn_setup():
        import jax, jax.numpy as jnp
        import numpy as np
        E = 8
        TOP_K = 2
        D = 256
        M = 896
        B, S = (2, 256)
        key = jax.random.key(seed)
        kx, kg, k1, k2, k3 = jax.random.split(key, 5)
        x = jax.random.normal(kx, (B, S, D), dtype=jnp.float32)
        gate_w = jax.random.normal(kg, (D, E), dtype=jnp.float32) / np.sqrt(D)
        w1 = jax.random.normal(k1, (E, D, M), dtype=jnp.float32) / np.sqrt(D)
        w2 = jax.random.normal(k2, (E, M, D), dtype=jnp.float32) / np.sqrt(M)
        w3 = jax.random.normal(k3, (E, D, M), dtype=jnp.float32) / np.sqrt(D)
        return {'x': x, 'gate_w': gate_w, 'w1': w1, 'w2': w2, 'w3': w3}
    _L0_ffn_all = _L0_ffn_setup()
    _L0_ffn_in = {k: v for k, v in _L0_ffn_all.items() if k in ('gate_w', 'w1', 'w2', 'w3')}
    del _L0_ffn_all

    def _L1_xattn_setup():
        import jax, jax.numpy as jnp
        import numpy as np
        H = 256
        NH = 16
        HD = H // NH
        EPS = 1e-06

        def rmsnorm(x, w, eps=EPS):
            var = jnp.mean(x * x, axis=-1, keepdims=True)
            return x * jax.lax.rsqrt(var + eps) * w
        key = jax.random.key(seed)
        ks = jax.random.split(key, 9)
        B, L, M = (4, 512, 32)
        s = 1.0 / np.sqrt(H)
        return {'hidden_states': jax.random.normal(ks[0], (B, L, H), dtype=jnp.float32), 'memory_tokens': jax.random.normal(ks[1], (B, M, H), dtype=jnp.float32), 'memory_mask': jax.random.randint(ks[2], (B, M), 0, 2).astype(bool), 'norm_w': jnp.ones((H,), dtype=jnp.float32), 'wq': jax.random.normal(ks[3], (H, H), dtype=jnp.float32) * s, 'wk': jax.random.normal(ks[4], (H, H), dtype=jnp.float32) * s, 'wv': jax.random.normal(ks[5], (H, H), dtype=jnp.float32) * s, 'wo': jax.random.normal(ks[6], (H, H), dtype=jnp.float32) * s, 'wg': jax.random.normal(ks[7], (H, H), dtype=jnp.float32) * s}
    _L1_xattn_all = _L1_xattn_setup()
    _L1_xattn_in = {k: v for k, v in _L1_xattn_all.items() if k in ('norm_w', 'wq', 'wk', 'wv', 'wo', 'wg')}
    del _L1_xattn_all

    def _L1_ffn_setup():
        import jax, jax.numpy as jnp
        import numpy as np
        TOPK = 4
        key = jax.random.key(seed)
        k_x, k_a, k_b, k_w, k_bias = jax.random.split(key, 5)
        b, s, h, j, a, r = (4, 256, 256, 256, 64, 16)
        x = jax.random.normal(k_x, (b, s, h), dtype=jnp.float32)
        A = jax.random.normal(k_a, (a, r, h), dtype=jnp.float32) * 0.02
        B = jax.random.normal(k_b, (a, j, r), dtype=jnp.float32) * 0.02
        W = jax.random.normal(k_w, (j, h), dtype=jnp.float32) * 0.02
        bias = jax.random.normal(k_bias, (j,), dtype=jnp.float32) * 0.02
        return {'x': x, 'A': A, 'B': B, 'W': W, 'bias': bias}
    _L1_ffn_all = _L1_ffn_setup()
    _L1_ffn_in = {k: v for k, v in _L1_ffn_all.items() if k in ('A', 'B', 'W', 'bias')}
    del _L1_ffn_all
    return {'x': x, 'ctx_2048': ctx_2048, 'mask_BxS2_bk0': mask_BxS2_bk0, 'g_xattn': g_xattn, 'g_ffn': g_ffn, 'L0_ffn_gate_w': _L0_ffn_in['gate_w'], 'L0_ffn_w1': _L0_ffn_in['w1'], 'L0_ffn_w2': _L0_ffn_in['w2'], 'L0_ffn_w3': _L0_ffn_in['w3'], 'L1_xattn_norm_w': _L1_xattn_in['norm_w'], 'L1_xattn_wq': _L1_xattn_in['wq'], 'L1_xattn_wk': _L1_xattn_in['wk'], 'L1_xattn_wv': _L1_xattn_in['wv'], 'L1_xattn_wo': _L1_xattn_in['wo'], 'L1_xattn_wg': _L1_xattn_in['wg'], 'L1_ffn_A': _L1_ffn_in['A'], 'L1_ffn_B': _L1_ffn_in['B'], 'L1_ffn_W': _L1_ffn_in['W'], 'L1_ffn_bias': _L1_ffn_in['bias']}

def reference(x, ctx_2048, mask_BxS2_bk0, g_xattn, g_ffn, L0_ffn_gate_w, L0_ffn_w1, L0_ffn_w2, L0_ffn_w3, L1_xattn_norm_w, L1_xattn_wq, L1_xattn_wk, L1_xattn_wv, L1_xattn_wo, L1_xattn_wg, L1_ffn_A, L1_ffn_B, L1_ffn_W, L1_ffn_bias):
    import jax
    import jax.numpy as jnp

    def _L0_xattn_ref(x, weight):
        import jax, jax.numpy as jnp
        import numpy as np
        FP8_MAX = 448.0
        ACT_EPS = 0.0001
        W_EPS = 1e-06
        BLK = 128

        def quant_dequant_act_1x128(x):
            E, M, K = x.shape
            xb = x.reshape(E, M, K // BLK, BLK)
            amax = jnp.max(jnp.abs(xb), axis=-1, keepdims=True)
            safe = jnp.maximum(amax, ACT_EPS)
            q = (xb * (FP8_MAX / safe)).astype(jnp.float8_e4m3fn)
            return (q.astype(jnp.float32) * (safe / FP8_MAX)).reshape(E, M, K)

        def quant_dequant_weight_128x128(w):
            E, N, K = w.shape
            wb = w.reshape(E, N // BLK, BLK, K // BLK, BLK)
            amax = jnp.max(jnp.abs(wb), axis=(2, 4), keepdims=True)
            safe = jnp.maximum(amax, W_EPS)
            q = (wb * (FP8_MAX / safe)).astype(jnp.float8_e4m3fn)
            return (q.astype(jnp.float32) * (safe / FP8_MAX)).reshape(E, N, K)
        xq = quant_dequant_act_1x128(x)
        wq = quant_dequant_weight_128x128(weight)
        return jnp.einsum('emk,enk->emn', xq, wq)

    def _L0_ffn_ref(x, gate_w, w1, w2, w3):
        import jax, jax.numpy as jnp
        import numpy as np
        E = 8
        TOP_K = 2
        D = 256
        M = 896
        B, S = (2, 256)
        b, s, d = x.shape
        x_flat = x.reshape(-1, d)
        router_logits = x_flat @ gate_w
        router_probs = jax.nn.softmax(router_logits, axis=-1)
        topk_w, topk_idx = jax.lax.top_k(router_probs, TOP_K)
        topk_w = topk_w / jnp.sum(topk_w, axis=-1, keepdims=True)
        idx_flat = topk_idx.reshape(-1)
        sort_idx = jnp.argsort(idx_flat)
        x_rep_sort = jnp.take(x_flat, sort_idx // TOP_K, axis=0)
        group_sizes = jnp.bincount(idx_flat, length=E).astype(jnp.int32)
        h = jax.lax.ragged_dot(x_rep_sort, w1, group_sizes)
        h = jax.nn.silu(h) * jax.lax.ragged_dot(x_rep_sort, w3, group_sizes)
        out_sort = jax.lax.ragged_dot(h, w2, group_sizes)
        inv_sort_idx = jnp.argsort(sort_idx)
        out_rep = jnp.take(out_sort, inv_sort_idx, axis=0).reshape(-1, TOP_K, d)
        out = jnp.einsum('tkd,tk->td', out_rep, topk_w)
        return out.reshape(b, s, d)

    def _L1_xattn_ref(hidden_states, memory_tokens, memory_mask, norm_w, wq, wk, wv, wo, wg):
        import jax, jax.numpy as jnp
        import numpy as np
        H = 256
        NH = 16
        HD = H // NH
        EPS = 1e-06

        def rmsnorm(x, w, eps=EPS):
            var = jnp.mean(x * x, axis=-1, keepdims=True)
            return x * jax.lax.rsqrt(var + eps) * w
        B, L, C = hidden_states.shape
        M = memory_tokens.shape[1]
        scale = HD ** (-0.5)
        x = rmsnorm(hidden_states, norm_w)
        q = (x @ wq.T).reshape(B, L, NH, HD)
        k = (memory_tokens @ wk.T).reshape(B, M, NH, HD)
        v = (memory_tokens @ wv.T).reshape(B, M, NH, HD)
        attn = jnp.einsum('blhd,bmhd->bhlm', q, k) * scale
        attn = jnp.where(memory_mask[:, None, None, :], attn, -jnp.inf)
        attn = jax.nn.softmax(attn, axis=-1)
        attn = jnp.nan_to_num(attn, nan=0.0)
        out = jnp.einsum('bhlm,bmhd->blhd', attn, v).reshape(B, L, C)
        out = out @ wo.T
        gate = jax.nn.sigmoid(x @ wg.T)
        return gate * out

    def _L1_ffn_ref(x, A, B, W, bias):
        import jax, jax.numpy as jnp
        import numpy as np
        TOPK = 4
        vecs = jnp.einsum('arh,bsh->bsar', A, x)
        arrows = jnp.linalg.norm(vecs, axis=-1)
        _, idx = jax.lax.top_k(arrows, TOPK)
        routes = jax.nn.one_hot(idx, arrows.shape[-1], dtype=x.dtype).sum(-2) / TOPK
        v = jnp.einsum('bsa,bsar->bsr', routes, vecs)
        delta = jnp.einsum('bsa,ajr,bsr->bsj', routes, B, v)
        base = jnp.einsum('bsh,jh->bsj', x, W) + bias
        return base + delta
    x = x + jnp.tanh(g_xattn[0]) * _L0_xattn_ref(_layernorm(x, axis=-1), ctx_2048)
    x = x + jnp.tanh(g_ffn[0]) * _L0_ffn_ref(_layernorm(x, axis=-1), L0_ffn_gate_w, L0_ffn_w1, L0_ffn_w2, L0_ffn_w3)
    x = x + jnp.tanh(g_xattn[1]) * _L1_xattn_ref(_layernorm(x, axis=-1), ctx_2048, mask_BxS2_bk0, L1_xattn_norm_w, L1_xattn_wq, L1_xattn_wk, L1_xattn_wv, L1_xattn_wo, L1_xattn_wg)
    x = x + jnp.tanh(g_ffn[1]) * _L1_ffn_ref(_layernorm(x, axis=-1), L1_ffn_A, L1_ffn_B, L1_ffn_W, L1_ffn_bias)
    return x

_drawn_inputs = setup_inputs


def setup_inputs(seed=0):
    import zlib

    import numpy as np

    out = dict(_drawn_inputs(seed))
    spreads = {'g_ffn': (-1.0, 0.6), 'L1_xattn_norm_w': (1.0, 0.6)}
    factors = {'L1_xattn_wq': 8.0,
     'L1_xattn_wk': 8.0,
     'L1_xattn_wv': 8.0,
     'L1_xattn_wo': 8.0,
     'L1_xattn_wg': 8.0,
     'L1_ffn_A': 6.442,
     'L1_ffn_B': 5.315,
     'L1_ffn_bias': 3.93}
    for name, (base, spread) in spreads.items():
        noise = np.random.default_rng([zlib.crc32(name.encode()), seed]).standard_normal(out[name].shape)
        drawn = base * np.exp(spread * noise) if base else spread * noise
        out[name] = jnp.asarray(drawn.astype(out[name].dtype))
    for name, factor in factors.items():
        out[name] = (out[name] * factor).astype(out[name].dtype)
    return out
```

```python
from contextlib import ExitStack

import concourse.bass as bass
from concourse import mybir
from concourse.alu_op_type import AluOpType as ALU

ACT = mybir.ActivationFunctionType
F32 = mybir.dt.float32
BF16 = mybir.dt.bfloat16
I32 = mybir.dt.int32
U32 = mybir.dt.uint32
U8 = mybir.dt.uint8
AX_X = mybir.AxisListType.X
RMAX = bass.bass_isa.ReduceOp.max

P = 128
B, S, D = 4, 256, 256
T = B * S // P
TB = S // P
KD = D // P
FP8_MAX, ACT_EPS, W_EPS = 448.0, 1e-4, 1e-6
LN_EPS, RMS_EPS = 1e-5, 1e-6

E_N, M_F, TOPK = 8, 896, 2
MH = M_F // 2
JF = M_F // P
NT = (B * S * TOPK - E_N) // P + E_N
NTP = NT + 1
WE = 2 * KD * M_F + JF * D
LATE = 4

BANK = 512

NH, HD = 16, 16
ATT_SCALE = HD ** -0.5
HC = 4
NC = NH // HC
Q_PART = (0, 0, 1, 1, 0, 2)
K_PART = (0, 1, 0, 1, 2, 0)
ROWS_QK = 6 * HD
ROWS_S, ROWS_ST = ROWS_QK + 1, ROWS_QK + 4
MASKED, NO_KEY = -1e30, 1e29

NA, NR, RTOP = 64, 16, 4
AR = NA * NR
JA = AR // P


def bc(ap, n):
    return ap.unsqueeze(2).to_broadcast([ap.shape[0], ap.shape[1], n])


def flamingo(nc, a):
    out = a["out"]
    ctx = ExitStack()
    with ctx:
        def sb(name, shape, dt=F32):
            return ctx.enter_context(nc.sbuf_tensor(name, shape, dt))

        def sem(name):
            return ctx.enter_context(nc.semaphore(name))

        def dram(name, shape, dt=F32):
            return nc.dram_tensor(name, shape, dt, kind="Internal").ap()

        X = sb("X", [P, T, D])
        W = sb("W", [P, E_N * WE])
        SCR = sb("SCR", [P, 4608])
        ident = sb("ident", [P, P])
        ident_bf = sb("ident_bf", [P, P], BF16)
        ones_bf = sb("ones_bf", [P, P], BF16)
        before_bf = sb("before_bf", [P, P], BF16)
        iota_lane = sb("iota_lane", [P, P])
        pcol = sb("pcol", [P, 1])
        eps_ln = sb("eps_ln", [P, 1])
        gates = sb("gates", [P, 4])
        tg = sb("tg", [P, 4])
        stats = sb("stats", [P, T, 6])
        mv = sb("mv", [P, T, 2])
        rstd = sb("rstd", [P, T])
        SM = sb("SM", [P, 2300])

        PS = ctx.enter_context(nc.psum_tensor("PS", [P, 8 * BANK], F32))
        psum = [PS[:, i * BANK:(i + 1) * BANK] for i in range(8)]
        psbf = [x.bitcast(BF16) for x in psum]

        at = [0]

        def small(n):
            at[0] += n
            assert at[0] <= SM.shape[1]
            return SM[:, at[0] - n:at[0]]

        NB = T * KD
        amax_x, amax_c, amax_ca = small(NB), small(NB), small(NB)
        qs_x, qs_c, ds_x, ds_c = small(NB), small(NB), small(NB), small(NB)
        coef = small(T * KD * TB).rearrange("p (t k n) -> p t k n", t=T, k=KD)
        logits_v = small(T * E_N)
        top8 = small(T * 8)
        top8i = small(T * 8).bitcast(U32)
        top8f = small(T * 8)
        onehot = small(T * TOPK * E_N)
        hits = small(T * E_N)
        hits_bf = small(T * E_N // 2).bitcast(BF16)
        wtk = small(T * TOPK)
        tiles_e, tiles_c, base_e, ones8 = small(E_N), small(E_N), small(E_N), small(E_N)
        cmp64 = small(64)
        slot_e = small(T * E_N)
        prod = small(T * TOPK * E_N)
        slot_f, lane_f, tile_f = small(T * TOPK), small(T * TOPK), small(T * TOPK)
        slot_i, lane_i, tile_i = (small(T * TOPK).bitcast(I32) for _ in range(3))
        tile_no = small(NTP)
        tok_f, tok_i = small(NTP), small(NTP).bitcast(I32)
        eid_f, eid_i = small(NTP), small(NTP).bitcast(I32)
        idx_col = small(2).bitcast(I32)

        def wt(e):
            return W[:, e * WE:(e + 1) * WE]

        late = [(E_N - LATE) * WE]

        def early(n):
            late[0] += n
            assert late[0] <= E_N * WE
            return W[:, late[0] - n:late[0]]

        ctx_rows, xn, xs, mag, cs = (early(T * D) for _ in range(5))
        kv_raw = early(2 * KD * D).rearrange("p (w t d) -> p w t d", w=2, t=KD)
        kv_wT = early(2 * KD * D).rearrange("p (w k c) -> p w k c", w=2, k=KD)
        ctxT = early(KD * B * S).rearrange("p (k t) -> p k t", k=KD)
        k32 = early(KD * B * S)
        k_parts = early(3 * KD * B * S // 2).bitcast(BF16).rearrange("p (j n) -> p j n", j=3)
        v32 = early(T * D)
        post = [0]

        def room(n):
            post[0] += n
            assert post[0] <= E_N * WE
            return W[:, post[0] - n:post[0]]

        yk = room(T * TOPK * D).rearrange("p (n d) -> p n d", d=D)
        q_parts = yk.rearrange("p n d -> p (n d)")[:, 0:3 * KD * B * S // 2].bitcast(BF16).rearrange("p (j n) -> p j n", j=3)
        l1_raw = room(3 * KD * D).rearrange("p (w t d) -> p w t d", w=3, t=KD)
        wo_wide = room(KD * NH * 32).rearrange("p (t h w) -> p t h w", t=KD, h=NH)
        qg_wT = room(2 * KD * D).rearrange("p (w k c) -> p w k c", w=2, k=KD)
        wo_wT = room(NC * D).rearrange("p (c n) -> p c n", c=NC)
        Qp = room(NH * B * S // 2).bitcast(BF16).rearrange("p (h t) -> p h t", h=NH)
        Kp = room(NH * B * S // 2).bitcast(BF16).rearrange("p (h t) -> p h t", h=NH)
        v_wide = room(TB * NH * 32).rearrange("p (m h w) -> p m h w", m=TB, h=NH)
        v_rows = room(T * D)
        probs_w = room(3 * 1024)
        probs = [probs_w[:, i * 1024:(i + 1) * 1024].rearrange("p (g m l) -> p g m l", g=2, m=TB) for i in range(2)]
        q_rest = [probs_w[:, 2048 + i * BANK:2048 + (i + 1) * BANK] for i in range(2)]
        b_raw = probs_w[:, 0:2048].rearrange("p (j n) -> p j n", j=KD)
        gate_s = room(T * D)
        attn = room(NC * S).rearrange("p (c l) -> p c l", c=NC)
        spare = room(NC * S)
        a_raw_w = W[:, post[0] - 2 * NC * S:post[0]]
        a_raw = a_raw_w.rearrange("p (j d) -> p j d", j=JA)
        rec, rec_s = room(S), room(S)
        o_tmp = spare[:, 0:TB * D]
        w_raw = room(KD * D).rearrange("p (t d) -> p t d", t=KD)
        aT = room(KD * AR).rearrange("p (k n) -> p k n", k=KD)
        bT = room(JA * D).rearrange("p (j d) -> p j d", j=JA)
        wT = room(KD * D).rearrange("p (k n) -> p k n", k=KD)
        x3n = SCR[:, 0:T * D]
        x3T = SCR[:, T * D:2 * T * D].rearrange("p (k t) -> p k t", k=KD)
        def f_room(at, n):
            return Qp.rearrange("p h t -> p (h t)").bitcast(F32)[:, at:at + n]

        x4n = [f_room(i * D, D) for i in range(2)]
        x4T = [f_room(512 + i * D, D).rearrange("p (k s) -> p k s", k=KD) for i in range(2)]
        vecs2 = f_room(1024, AR)
        picked = f_room(2048, AR)
        u_s = f_room(3072, AR)
        uT = f_room(4096, AR).rearrange("p (j s) -> p j s", j=JA)
        norm2 = f_room(5120, NA)
        f_top = f_room(5184, 8)
        f_topi = f_room(5192, 8).bitcast(U32)
        f_topf = f_room(5200, 8)
        routes = f_room(5208, NA)
        v_sum = f_room(5272, NR)
        nw = small(KD)
        rms = small(T)
        mx = small(TB * NH).rearrange("p (t h) -> p t h", t=TB)
        mneg = small(TB * NH).rearrange("p (t h) -> p t h", t=TB)
        mparts = small(TB * 3 * NH // 2).bitcast(BF16).rearrange("p (t j h) -> p t j h", t=TB, j=3)
        mT = small(S // 2).bitcast(BF16)
        bias_row = small(D)
        mask_u8 = small(B * S // 4).bitcast(U8)[0:1, :]
        mask_row = ctxT.rearrange("p k t -> p (k t)")[0:1, 0:B * S // 2].bitcast(BF16)
        one_row = ctxT.rearrange("p k t -> p (k t)")[0:1, B * S // 2:B * S].bitcast(BF16)
        ones_row = small(P)
        qx_bf = SCR[:, 0:1024].bitcast(BF16)
        qc_bf = SCR[:, 1024:2048].bitcast(BF16)
        qxT = SCR[:, 2048:3072].bitcast(BF16).rearrange("p (k t) -> p k t", k=KD)
        qcT = SCR[:, 3072:4096].bitcast(BF16).rearrange("p (k t) -> p k t", k=KD)
        xnT = xs.rearrange("p (k t) -> p k t", k=KD)
        gate_w = SCR[:, 4096:4096 + KD * E_N].rearrange("p (k e) -> p k e", k=KD)
        oh_lane = mag.bitcast(BF16)[:, 0:T * TOPK * P].rearrange("p (n l) -> p n l", l=P)
        oh_tile = cs[:, 0:T * TOPK * NTP].rearrange("p (n l) -> p n l", l=NTP)
        ohv = cs[:, 512:512 + T * TOPK * NTP].bitcast(BF16).rearrange("p (n two l) -> p n two l", two=2, l=NTP)
        xg = [SCR[:, i * D:(i + 1) * D] for i in range(2)]
        xgT = [SCR[:, 512 + i * D:512 + (i + 1) * D].rearrange("p (k s) -> p k s", k=KD) for i in range(2)]
        g_s = SCR[:, 1024:1024 + M_F]
        hm = SCR[:, 1920:1920 + M_F]
        hT = SCR[:, 2816:2816 + M_F].rearrange("p (j s) -> p j s", j=JF)
        ys = [SCR[:, 3712 + i * D:3712 + (i + 1) * D] for i in range(2)]
        assert 3712 + 2 * D <= SCR.shape[1]

        XN_d = dram("xn_rows", [B * S, D])
        KP_d = dram("key_parts", [3, D, B * S], BF16)
        QP_d = dram("query_parts", [3, D, B * S], BF16)
        V_d = dram("values", [B * S, D])
        ROW_d = dram("mask_and_one_rows", [2, B * S], BF16)
        YS_d = dram("slot_rows", [NT * P, D])

        s_x, s_c, s_g, s_gw = sem("x_landed"), sem("ctx_landed"), sem("gates_landed"), sem("gate_w_landed")
        s_w = [sem(f"expert{e}_landed") for e in range(E_N)]
        s_wr = sem("experts_ready")
        s_const = sem("constants_made")
        s_poolc = sem("pool_steps")
        s_v = sem("vector_steps")
        s_a = sem("scalar_steps")
        s_tg = sem("tanh_done")
        s_var = sem("variance_done")
        s_std = sem("std_done")
        s_amaxc = sem("ctx_block_max_done")
        s_allc = sem("ctx_max_over_partitions")
        s_qc, s_qx = sem("ctx_quantised"), sem("x_quantised")
        s_tr = sem("q_transposed")
        s_trc = sem("q_transposes_copied")
        s_xa = sem("cross_products_done")
        s_xn2 = sem("xn2_done")
        s_x2T, s_x2Tc = sem("xn2_transposed"), sem("xn2_transposes_copied")
        s_rt = sem("logits_done")
        s_hits = sem("hits_done")
        s_rank = sem("ranks_done")
        s_dl, s_ed = sem("logit_gap_done"), sem("gap_exp_done")
        s_oh = sem("slot_onehots_done")
        s_tokp = sem("slot_tokens_done")
        s_tab = sem("tile_tables_done")
        s_free2 = sem("last_experts_room_free")
        s_xnd = sem("xn_rows_stored")
        s_rows = [sem(f"rows_landed{i}") for i in range(2)]
        s_idx = sem("index_copied")
        s_xTp, s_xTs = sem("xT_in_psum"), sem("xT_in_sbuf")
        s_h1, s_h3 = sem("h1_done"), sem("h3_done")
        s_gs = sem("silu_done")
        s_hm = sem("hidden_done")
        s_hTp, s_hTs = sem("hT_in_psum"), sem("hT_in_sbuf")
        s_y, s_ys = sem("y_done"), sem("y_in_sbuf")
        s_st = [sem(f"y_stored{i}") for i in range(2)]
        s_yk = sem("slot_rows_fetched")
        s_out = sem("out_stored")

        s_kvw, s_mask = sem("kv_weights_landed"), sem("mask_landed")
        s_kvT, s_kvTc = sem("kv_transposed"), sem("kv_transposes_copied")
        s_kv, s_kvc = sem("kv_products_done"), sem("kv_products_copied")
        s_kpart = sem("key_parts_made")
        s_maskrow = sem("mask_row_made")
        s_kvst = sem("kv_stored")
        s_prew = sem("layer1_weights_landed")
        s_ffw = sem("ffn1_weights_landed")
        s_kp = sem("keys_packed")
        s_vr = sem("values_landed")
        s_wop = sem("wo_widened")
        s_l1T, s_l1Tc = sem("layer1_weights_transposed"), sem("layer1_transposes_copied")
        s_x3n = sem("x3n_done")
        s_x3T, s_x3Tc = sem("x3n_transposed"), sem("x3n_transposes_copied")
        s_q, s_qh, s_qr, s_qp = sem("q_done"), sem("q_high_done"), sem("q_read"), sem("q_parts_done")
        s_qst, s_qpk = sem("q_parts_stored"), sem("q_packed")
        s_gt, s_gtc = sem("gate_product_done"), sem("gate_done")
        s_gsc = sem("gate_scaled")
        s_S, s_mx = sem("scores_done"), sem("score_max_done")
        s_nm, s_nmp, s_nmc, s_nmd = sem("max_parts_done"), sem("max_transposed"), sem("max_copied"), sem("max_rows_landed")
        s_ST, s_pt = sem("scoresT_done"), sem("probs_done")
        s_PV, s_at = sem("pv_done"), sem("attn_normalised")
        s_vw = sem("values_widened")
        chain, chain2, chain3, chain4 = (sem(x) for x in ("max_part_steps", "normalise_steps", "out_steps", "route_steps"))
        s_O, s_oe = sem("o_done"), sem("o_added")
        s_xf, s_fT, s_fTc = sem("x4n_done"), sem("x4n_transposed"), sem("x4n_transposes_copied")
        s_V, s_sq, s_ar, s_pk = sem("vecs_done"), sem("squares_done"), sem("squares_read"), sem("vecs_read")
        s_u, s_uT, s_uTc = sem("u_done"), sem("u_transposed"), sem("u_transposes_copied")
        s_alone = sem("waits_that_stand_alone")
        s_D, s_fin = sem("ffn1_done"), sem("tile_final")

        block = ctx.enter_context(nc.Block())

        @block.sync
        def _(sp):
            sp.dma_start(X[:, :, :], a["x"].rearrange("b (t p) d -> p (b t) d", p=P)).then_inc(s_x, 16)
            sp.dma_start(ctx_rows.rearrange("p (t d) -> p t d", d=D),
                         a["ctx_2048"].rearrange("b (t p) d -> p (b t) d", p=P)).then_inc(s_c, 16)
            sp.dma_start(gates[:, 0:2], a["g_xattn"].unsqueeze(0).to_broadcast([P, 2])).then_inc(s_g, 16)
            sp.dma_start(gates[:, 2:4], a["g_ffn"].unsqueeze(0).to_broadcast([P, 2])).then_inc(s_g, 16)
            sp.dma_start(gate_w, a["L0_ffn_gate_w"].rearrange("(k p) e -> p k e", p=P)).then_inc(s_gw, 16)

            for n, w in enumerate(("L1_xattn_wk", "L1_xattn_wv")):
                sp.dma_start(kv_raw[:, n, :, :], a[w].rearrange("(t p) d -> p t d", p=P)).then_inc(s_kvw, 16)
            sp.dma_start(mask_u8, a["mask_BxS2_bk0"].rearrange("b s -> (b s)").unsqueeze(0)).then_inc(s_mask, 16)
            sp.dma_start(nw, a["L1_xattn_norm_w"].rearrange("(k p) -> p k", p=P), allow_slow_non_contiguous=True).then_inc(s_mask, 16)
            sp.dma_start(bias_row[0:1, :], a["L1_ffn_bias"].unsqueeze(0)).then_inc(s_mask, 16)

            def load_expert(e):
                h = KD * M_F
                for n, w in enumerate(("L0_ffn_w1", "L0_ffn_w3")):
                    sp.dma_start(wt(e)[:, n * h:(n + 1) * h].rearrange("p (k f) -> p k f", k=KD),
                                 a[w][e].rearrange("(k p) f -> p k f", p=P)).then_inc(s_w[e], 16)
                sp.dma_start(wt(e)[:, 2 * h:WE].rearrange("p (j d) -> p j d", j=JF),
                             a["L0_ffn_w2"][e].rearrange("(j p) d -> p j d", p=P)).then_inc(s_w[e], 16)

            for e in range(E_N - LATE):
                load_expert(e)
            sp.wait_ge(s_kpart, 3)
            sp.dma_start(KP_d.rearrange("j (c p) t -> p (j c) t", p=P),
                         k_parts.rearrange("p j (c t) -> p (j c) t", c=KD)).then_inc(s_kvst, 16)
            sp.wait_ge(s_kvc, 8)
            sp.dma_start(V_d.rearrange("(t p) d -> p t d", p=P), v32.rearrange("p (t d) -> p t d", d=D)).then_inc(s_kvst, 16)
            sp.wait_ge(s_maskrow, 1)
            sp.dma_start(ROW_d[0:1, :], mask_row).then_inc(s_kvst, 16)
            sp.dma_start(ROW_d[1:2, :], one_row).then_inc(s_kvst, 16)
            sp.wait_ge(s_xn2, 1)
            sp.dma_start(XN_d.rearrange("(t p) d -> p t d", p=P), xn.rearrange("p (t d) -> p t d", d=D)).then_inc(s_xnd, 16)
            sp.wait_ge(s_free2, 1)
            sp.wait_ge(s_xnd, 16)
            sp.wait_ge(s_kvst, 64)
            for e in range(E_N - LATE, E_N):
                load_expert(e)
            for e in range(E_N):
                sp.wait_ge(s_w[e], 48)
                sp.sem_inc(s_wr, 1)
            sp.wait_ge(s_y, NT)
            for n, w in enumerate(("L1_xattn_wq", "L1_xattn_wg", "L1_xattn_wo")):
                sp.dma_start(l1_raw[:, n, :, :], a[w].rearrange("(t p) d -> p t d", p=P)).then_inc(s_prew, 16)
            sp.dma_start(a_raw, a["L1_ffn_A"].rearrange("a r d -> (a r) d").rearrange("(j p) d -> p j d", p=P)).then_inc(s_ffw, 16)
            sp.dma_start(w_raw, a["L1_ffn_W"].rearrange("(t p) d -> p t d", p=P)).then_inc(s_ffw, 16)
            for j in range(KD):
                sp.dma_start(b_raw[:, j, :].rearrange("p (a r) -> p a r", r=NR),
                             a["L1_ffn_B"][:, j * P:(j + 1) * P, :].rearrange("a p r -> p a r")).then_inc(s_ffw, 16)
            for n, j in enumerate(K_PART):
                sp.dma_start(Kp[n * HD:(n + 1) * HD, :, :], KP_d[j].rearrange("(h d) t -> d h t", d=HD)).then_inc(s_kp, 16)
            sp.dma_start(Kp[ROWS_QK:ROWS_S, :, :], ROW_d[0:1, :].unsqueeze(1).to_broadcast([1, NH, B * S])).then_inc(s_kp, 16)
            for r in range(ROWS_S, ROWS_ST):
                sp.dma_start(Kp[r:r + 1, :, :], ROW_d[1:2, :].unsqueeze(1).to_broadcast([1, NH, B * S])).then_inc(s_kp, 16)
            sp.dma_start(Qp[ROWS_QK:ROWS_S, :, :], ROW_d[1:2, :].unsqueeze(1).to_broadcast([1, NH, B * S])).then_inc(s_kp, 16)
            sp.dma_start(v_rows.rearrange("p (t d) -> p t d", d=D), V_d.rearrange("(t p) d -> p t d", p=P)).then_inc(s_vr, 16)
            sp.wait_ge(s_qp, 4)
            sp.dma_start(QP_d.rearrange("j (c p) t -> p (j c) t", p=P),
                         q_parts.rearrange("p j (c t) -> p (j c) t", c=KD)).then_inc(s_qst, 16)
            sp.wait_ge(s_qst, 16)
            for n, j in enumerate(Q_PART):
                sp.dma_start(Qp[n * HD:(n + 1) * HD, :, :], QP_d[j].rearrange("(h d) t -> d h t", d=HD)).then_inc(s_qpk, 16)

            def max_rows(b):
                sp.wait_ge(s_nmc, b + 1)
                for j in range(3):
                    sp.dma_start(Qp[ROWS_S + j:ROWS_S + j + 1, :, bass.ds(b * S, S)], mT[j * NH:(j + 1) * NH, :]).then_inc(s_nmd, 16)

            max_rows(0)
            with sp.Fori(1, B) as b:
                max_rows(b)

            def store(t):
                sp.wait_ge(s_fin, t + 1)
                sp.dma_start(out.rearrange("b s d -> (b s) d")[bass.ds(t * P, P), :], X[:, bass.ds(t, 1), :].rearrange("p t d -> p (t d)")).then_inc(s_out, 16)

            with sp.Fori(0, T) as t:
                store(t)
            sp.wait_ge(s_out, 16 * T)

        @block.gpsimd
        def _(pool):
            steps = [0]

            def link(ins):
                steps[0] += 1
                ins.then_inc(s_poolc, 1)
                pool.wait_ge(s_poolc, steps[0])

            nc.gpsimd.memset(ident_bf[:, :], 0.0)
            nc.gpsimd.memset(ones_bf[:, :], 1.0)
            link(nc.gpsimd.memset(ident[:, :], 0.0))
            nc.gpsimd.affine_select(out=ident[:, :], in_=ident[:, :], compare_op=ALU.not_equal, fill=1.0,
                                    base=0, pattern=[[-1, P]], channel_multiplier=1)
            nc.gpsimd.affine_select(out=ident_bf[:, :], in_=ident_bf[:, :], compare_op=ALU.not_equal, fill=1.0,
                                    base=0, pattern=[[-1, P]], channel_multiplier=1)
            nc.gpsimd.affine_select(out=before_bf[:, :], in_=ones_bf[:, :], compare_op=ALU.is_ge, fill=0.0,
                                    base=-1, pattern=[[1, P]], channel_multiplier=-1)
            nc.gpsimd.iota(iota_lane[:, :], pattern=[[1, P]], base=0, channel_multiplier=0,
                           allow_small_or_imprecise_dtypes=True)
            nc.gpsimd.iota(tile_no, pattern=[[1, NTP]], base=0, channel_multiplier=0,
                           allow_small_or_imprecise_dtypes=True)
            nc.gpsimd.iota(cmp64.rearrange("p (e j) -> p e j", e=E_N), pattern=[[0, E_N], [P, T]], base=0, channel_multiplier=0,
                           allow_small_or_imprecise_dtypes=True)
            nc.gpsimd.iota(pcol[:, :], pattern=[[0, 1]], base=0, channel_multiplier=1,
                           allow_small_or_imprecise_dtypes=True).then_inc(s_const, 1)
            pool.wait_ge(s_amaxc, 1)
            nc.gpsimd.partition_all_reduce(amax_ca, amax_c, P, RMAX).then_inc(s_allc, 1)

            for c in range(KD):
                half = slice(c * B * S, (c + 1) * B * S)
                pool.wait_ge(s_kvc, 2 * c + 2)
                link(nc.gpsimd.tensor_copy(k_parts[:, 0, half], k32[:, half]))
                link(nc.gpsimd.tensor_tensor(k32[:, half], k32[:, half], k_parts[:, 0, half], ALU.subtract))
                link(nc.gpsimd.tensor_copy(k_parts[:, 1, half], k32[:, half]))
                nc.gpsimd.tensor_tensor(k_parts[:, 2, half], k32[:, half], k_parts[:, 1, half], ALU.subtract).then_inc(s_kpart, 1)
            nc.gpsimd.memset(ones_row[0:1, :], 1.0).then_inc(s_kpart, 1)

            pool.wait_ge(s_tab, 1)
            pool.wait_ge(s_xnd, 16)

            def fetch(i, u, n):
                if n is not None:
                    pool.wait_ge(s_xTp, n)
                nc.gpsimd.tensor_copy(idx_col[:, u:u + 1], tok_i[:, bass.ds(i, 1)]).then_inc(s_idx, 1)
                pool.wait_ge(s_idx, i + 1)
                pool.sem_inc(s_alone, 1)
                nc.gpsimd.indirect_dma_start(xg[u], None, XN_d[:, :], bass.IndirectOffsetOnAxis(ap=idx_col[:, u:u + 1], axis=0)).then_inc(s_rows[u], 16)

            fetch(0, 0, None)
            fetch(1, 1, None)
            with pool.Fori(2, NT - 1, 2) as i:
                fetch(i, 0, i - 1)
                fetch(i + 1, 1, i)
            fetch(NT - 1, 0, NT - 2)

            for u in range(2):
                pool.wait_ge(s_st[u], 16 * ((NT + 1 - u) // 2))
            for n in range(T * TOPK):
                nc.gpsimd.indirect_dma_start(yk[:, n, :], None, YS_d[:, :],
                                             bass.IndirectOffsetOnAxis(ap=slot_i[:, n:n + 1], axis=0)).then_inc(s_yk, 16)
            link(nc.gpsimd.memset(v_wide, 1.0))
            link(nc.gpsimd.memset(wo_wide, 0.0))
            pool.wait_ge(s_prew, 48)
            nc.gpsimd.tensor_copy(wo_wide[:, :, :, 0:HD], l1_raw[:, 2, :, :].rearrange("p t (h d) -> p t h d", d=HD)).then_inc(s_wop, 1)

            def widen_values(b):
                nc.gpsimd.tensor_copy(v_wide[:, :, :, 0:HD],
                                      v_rows[:, bass.ds(b * TB * D, TB * D)].rearrange("p (m h d) -> p m h d", m=TB, d=HD)).then_inc(s_vw, 1)

            pool.wait_ge(s_vr, 16)
            widen_values(0)
            pool.wait_ge(s_gtc, 4)
            nc.gpsimd.tensor_scalar(gate_s, gate_s, tg[:, 1:2], None, ALU.mult).then_inc(s_gsc, 1)
            with pool.Fori(1, B) as b:
                pool.wait_ge(s_PV, b * 8)
                widen_values(b)

        @block.scalar
        def _(act):
            act.wait_ge(s_g, 32)
            nc.scalar.activation(tg[:, :], gates[:, :], ACT.Tanh).then_inc(s_tg, 1)
            act.wait_ge(s_var, 1)
            nc.scalar.activation(rstd[:, :], mv[:, :, 1], ACT.Sqrt, bias=eps_ln[:, 0:1]).then_inc(s_std, 1)
            act.wait_ge(s_kvT, 1)
            for n in range(2):
                nc.scalar.activation(kv_wT[:, n, :, :], psum[n].rearrange("p (k c) -> p k c", k=KD), ACT.Copy).then_inc(s_kvTc, 1)
            act.wait_ge(s_kvT, 2)
            for n in range(4):
                nc.scalar.activation(ctxT[:, n // 2, (n % 2) * BANK:(n % 2 + 1) * BANK], psum[2 + n], ACT.Copy).then_inc(s_kvTc, 1)
            for n, bank in enumerate((0, 1, 6, 7)):
                act.wait_ge(s_kv, n + 1)
                nc.scalar.activation(k32[:, n * BANK:(n + 1) * BANK], psum[bank], ACT.Copy).then_inc(s_kvc, 1)
            for n in range(4):
                act.wait_ge(s_kv, n + 5)
                nc.scalar.activation(v32[:, n * BANK:(n + 1) * BANK], psum[2 + n], ACT.Copy).then_inc(s_kvc, 1)
            for g in range(2):
                act.wait_ge(s_tr, 2 * g + 1)
                for k in range(KD):
                    dst = (qcT, qxT)[g][:, k, :]
                    nc.scalar.activation(dst, psbf[4 * g + k][:, 0:T * P], ACT.Copy).then_inc(s_trc, 1)
            act.wait_ge(s_var, 2)
            nc.scalar.activation(rstd[:, :], mv[:, :, 1], ACT.Sqrt, bias=eps_ln[:, 0:1]).then_inc(s_std, 1)
            for n in range(4):
                act.wait_ge(s_x2T, n + 1)
                nc.scalar.activation(xnT[:, n // 2, (n % 2) * 512:(n % 2 + 1) * 512], psum[n][:, :], ACT.Copy).then_inc(s_x2Tc, 1)
            act.wait_ge(s_dl, 1)
            nc.scalar.activation(wtk[:, 0:T], wtk[:, 0:T], ACT.Exp).then_inc(s_ed, 1)

            def silu(i):
                act.wait_ge(s_h1, i + 1)
                act.wait_ge(s_hm, i)
                for h in range(2):
                    last = nc.scalar.activation(g_s[:, h * MH:(h + 1) * MH], psum[h][:, 0:MH], ACT.Silu)
                last.then_inc(s_gs, 1)

            def copy_xT(i, u):
                act.wait_ge(s_xTp, i + 1)
                nc.scalar.activation(xgT[u], psum[6][:, 0:D].rearrange("p (k s) -> p k s", k=KD), ACT.Copy).then_inc(s_xTs, 1)

            def store_y(i, u, before):
                act.wait_ge(s_y, i + 1)
                if before is not None:
                    act.wait_ge(s_st[u], 16 * before)
                nc.scalar.activation(ys[u], psum[7][:, 0:D], ACT.Copy).then_inc(s_ys, 1)
                act.wait_ge(s_ys, i + 1)
                act.dma_start(YS_d[bass.ds(i * P, P), :], ys[u]).then_inc(s_st[u], 16)

            copy_xT(0, 0)
            act.wait_ge(s_h1, 1)
            for h in range(2):
                last = nc.scalar.activation(g_s[:, h * MH:(h + 1) * MH], psum[h][:, 0:MH], ACT.Silu)
            last.then_inc(s_gs, 1)
            copy_xT(1, 1)
            silu(1)
            copy_xT(2, 0)
            store_y(0, 0, None)
            silu(2)
            copy_xT(3, 1)
            store_y(1, 1, None)
            with act.Fori(3, NT - 2, 2) as i:
                half = act.snap(i // 2)
                silu(i)
                copy_xT(i + 1, 0)
                store_y(i - 1, 0, half)
                silu(i + 1)
                copy_xT(i + 2, 1)
                store_y(i, 1, half)
            silu(NT - 2)
            copy_xT(NT - 1, 0)
            store_y(NT - 3, 0, (NT - 3) // 2)
            silu(NT - 1)
            store_y(NT - 2, 1, (NT - 2) // 2)
            store_y(NT - 1, 0, (NT - 1) // 2)

            act.wait_ge(s_l1T, 1)
            for n in range(2):
                nc.scalar.activation(qg_wT[:, n, :, :], psum[n].rearrange("p (k c) -> p k c", k=KD), ACT.Copy).then_inc(s_l1Tc, 1)
            act.wait_ge(s_l1T, 2)
            for n in range(2):
                nc.scalar.activation(wo_wT[:, 2 * n:2 * n + 2, :], psum[2 + n].rearrange("p (c o) -> p c o", c=2), ACT.Copy).then_inc(s_l1Tc, 1)
            act.wait_ge(s_l1T, 3)
            for n in range(4):
                nc.scalar.activation(aT[:, n // 2, (n % 2) * BANK:(n % 2 + 1) * BANK], psum[4 + n], ACT.Copy).then_inc(s_l1Tc, 1)
            act.wait_ge(s_l1T, 4)
            for n in range(4):
                nc.scalar.activation(bT[:, 2 * n:2 * n + 2, :], psum[4 + n].rearrange("p (j d) -> p j d", j=2), ACT.Copy).then_inc(s_l1Tc, 1)
            nc.scalar.activation(wT, psum[0].rearrange("p (k n) -> p k n", k=KD), ACT.Copy).then_inc(s_l1Tc, 1)
            for n in (3, 4):
                act.wait_ge(s_var, n)
                if n == 3:
                    nc.scalar.activation(rstd[:, :], mv[:, :, 1], ACT.Sqrt, bias=eps_ln[:, 0:1]).then_inc(s_std, 1)
                else:
                    nc.scalar.activation(rms, rms, ACT.Sqrt).then_inc(s_std, 1)
            for n in range(4):
                act.wait_ge(s_x3T, n + 1)
                nc.scalar.activation(x3T[:, n // 2, (n % 2) * BANK:(n % 2 + 1) * BANK], psum[n], ACT.Copy,
                                     scale=nw[:, n // 2:n // 2 + 1]).then_inc(s_x3Tc, 1)
            for n in range(4):
                act.wait_ge(s_q, n + 1)
                nc.scalar.activation(q_parts[:, 0, n * BANK:(n + 1) * BANK], psum[4 + n], ACT.Copy, scale=ATT_SCALE).then_inc(s_qh, 1)
            for n in range(4):
                act.wait_ge(s_gt, n + 1)
                nc.scalar.activation(gate_s[:, n * BANK:(n + 1) * BANK], psum[n], ACT.Sigmoid).then_inc(s_gtc, 1)

            def exps(b):
                for hp in range(NH // 2):
                    g = b * 8 + hp
                    act.wait_ge(s_ST, g + 1)
                    if not isinstance(g, int) or g >= 2:
                        act.wait_ge(s_PV, g - 1)
                    u = 2 + 2 * (hp % 2)
                    nc.scalar.activation(probs[hp % 2].rearrange("p g m l -> p (g m l)"), PS[:, u * BANK:(u + 2) * BANK], ACT.Exp).then_inc(s_pt, 1)

            exps(0)
            with act.Fori(1, B) as b:
                exps(b)

            act.wait_ge(s_var, 5)
            nc.scalar.activation(rstd[:, :], mv[:, :, 1], ACT.Sqrt, bias=eps_ln[:, 0:1]).then_inc(s_std, 1)

            def copy_x4T(t, u):
                act.wait_ge(s_fT, t + 1)
                nc.scalar.activation(x4T[u], psum[7][:, 0:D].rearrange("p (k s) -> p k s", k=KD), ACT.Copy).then_inc(s_fTc, 1)

            def squares(t, u):
                act.wait_ge(s_V, t + 1)
                if not isinstance(t, int) or t:
                    act.wait_ge(s_ar, t)
                nc.scalar.activation(vecs2, PS[:, 2 * u * BANK:(2 * u + 2) * BANK], ACT.Square).then_inc(s_sq, 1)

            def copy_uT(t):
                act.wait_ge(s_uT, t + 1)
                if not isinstance(t, int) or t:
                    act.wait_ge(s_D, t)
                nc.scalar.activation(uT, PS[:, 4 * BANK:6 * BANK].rearrange("p (j s) -> p j s", j=JA), ACT.Copy).then_inc(s_uTc, 1)

            def maps(t, u, ahead=2):
                if ahead >= 1:
                    squares(t + 1, 1 - u)
                copy_uT(t)
                if ahead >= 2:
                    copy_x4T(t + 2, u)

            copy_x4T(0, 0)
            squares(0, 0)
            copy_x4T(1, 1)
            maps(0, 0)
            with act.Fori(1, T - 3, 2) as t:
                maps(t, 1)
                maps(t + 1, 0)
            maps(T - 3, 1)
            maps(T - 2, 0, 1)
            maps(T - 1, 1, 0)

        @block.vector
        def _(v):
            steps = [0]

            def link(ins):
                steps[0] += 1
                ins.then_inc(s_v, 1)
                v.wait_ge(s_v, steps[0])

            def norm_stats(n):
                for t in range(T):
                    last = nc.vector.bn_stats(stats[:, t, :], X[:, t, :])
                link(last)
                for t in range(T):
                    last = nc.vector.bn_aggr(mv[:, t, :], stats[:, t, :])
                last.then_inc(s_var, 1)
                v.wait_ge(s_std, n)
                link(nc.vector.reciprocal(rstd[:, :], rstd[:, :]))

            def normalise(dst):
                for t in range(T):
                    last = nc.vector.tensor_scalar(dst[:, t * D:(t + 1) * D], X[:, t, :], mv[:, t, 0:1], rstd[:, t:t + 1],
                                                   ALU.subtract, ALU.mult)
                return last

            def block_scales(amax, eps, qs, ds):
                link(nc.vector.tensor_scalar(amax, amax, eps, None, ALU.max))
                nc.vector.tensor_scalar(ds, amax, 1.0 / FP8_MAX, None, ALU.mult)
                link(nc.vector.reciprocal(qs, amax))
                link(nc.vector.tensor_scalar(qs, qs, FP8_MAX, None, ALU.mult))

            def round_e4m3(src, qs, scaled, m, dst):
                link(nc.vector.tensor_tensor(scaled.rearrange("p (n l) -> p n l", l=P),
                                             src.rearrange("p (n l) -> p n l", l=P), bc(qs, P), ALU.mult))
                link(nc.vector.tensor_scalar(m.bitcast(I32), scaled.bitcast(I32), 0x7F800000, None, ALU.bitwise_and))
                link(nc.vector.tensor_scalar(m, m, 2.0 ** -6, 1.5 * 2.0 ** 20, ALU.max, ALU.mult))
                link(nc.vector.tensor_tensor(scaled, scaled, m, ALU.add))
                return nc.vector.tensor_tensor(dst, scaled, m, ALU.subtract)

            nc.vector.memset(ones8, 1.0)
            link(nc.vector.memset(eps_ln[:, :], LN_EPS))

            v.wait_ge(s_x, 16)
            norm_stats(1)
            v.wait_ge(s_c, 16)
            nc.vector.tensor_reduce(amax_c, ctx_rows.rearrange("p (n l) -> p n l", l=P), AX_X, ALU.max,
                                    apply_absolute_value=True).then_inc(s_amaxc, 1)
            link(normalise(xn))
            link(nc.vector.tensor_reduce(amax_x, xn.rearrange("p (n l) -> p n l", l=P), AX_X, ALU.max,
                                         apply_absolute_value=True))
            v.wait_ge(s_allc, 1)
            block_scales(amax_ca, W_EPS, qs_c, ds_c)
            round_e4m3(ctx_rows, qs_c, cs, mag, qc_bf).then_inc(s_qc, 1)
            v.wait_ge(s_qc, 1)
            block_scales(amax_x, ACT_EPS, qs_x, ds_x)
            round_e4m3(xn, qs_x, xs, mag, qx_bf).then_inc(s_qx, 1)
            v.wait_ge(s_tg, 1)
            link(nc.vector.tensor_scalar(ds_x, ds_x, tg[:, 0:1], None, ALU.mult))
            dsc = ds_c.rearrange("p (b n k) -> p b k n", b=B, n=TB)
            for t in range(T):
                last = nc.vector.tensor_tensor(coef[:, t, :, :], bc(ds_x[:, t * KD:(t + 1) * KD], TB), dsc[:, t // TB, :, :], ALU.mult)
            link(last)
            for t in range(T):
                v.wait_ge(s_xa, t + 1)
                for k in range(KD):
                    for n in range(TB):
                        dst = X[:, t, n * P:(n + 1) * P]
                        last = nc.vector.scalar_tensor_tensor(dst, psum[t][:, k * D + n * P:k * D + (n + 1) * P],
                                                              coef[:, t, k, n:n + 1], dst, ALU.mult, ALU.add)
                    if k < KD - 1 or t == T - 1:
                        link(last)

            v.wait_ge(s_mask, 48)
            v.wait_ge(s_kvc, 8)
            nc.vector.memset(one_row, 1.0)
            nc.vector.tensor_scalar(mask_row, mask_u8, -MASKED, MASKED, ALU.mult, ALU.add).then_inc(s_maskrow, 1)

            norm_stats(2)
            normalise(xn).then_inc(s_xn2, 1)
            v.wait_ge(s_rt, 1)
            link(nc.vector.tensor_copy(logits_v, psum[4][:, 0:T * E_N]))
            lg = logits_v.rearrange("p (t e) -> p t e", e=E_N)
            t8 = top8.rearrange("p (t e) -> p t e", e=8)
            t8i = top8i.rearrange("p (t e) -> p t e", e=8)
            t8f = top8f.rearrange("p (t e) -> p t e", e=8)
            for t in range(T):
                last = nc.vector.max(t8[:, t, :], lg[:, t, :])
            link(last)
            for t in range(T):
                last = nc.vector.max_index(t8i[:, t, :], t8[:, t, :], lg[:, t, :])
            link(last)
            nc.vector.tensor_tensor(wtk[:, 0:T], t8[:, :, 1], t8[:, :, 0], ALU.subtract).then_inc(s_dl, 1)
            link(nc.vector.tensor_copy(top8f, top8i))
            oh = onehot.rearrange("p (t k e) -> p t k e", t=T, k=TOPK)
            for k in range(TOPK):
                last = nc.vector.tensor_tensor(oh[:, :, k, :], iota_lane[:, 0:E_N].unsqueeze(1).to_broadcast([P, T, E_N]),
                                               bc(t8f[:, :, k], E_N), ALU.is_equal)
            link(last)
            nc.vector.tensor_tensor(hits_bf.rearrange("p (t e) -> p t e", e=E_N), oh[:, :, 0, :], oh[:, :, 1, :], ALU.add).then_inc(s_hits, 1)
            v.wait_ge(s_ed, 1)
            link(nc.vector.tensor_scalar(wtk[:, T:2 * T], wtk[:, 0:T], 1.0, None, ALU.add))
            link(nc.vector.reciprocal(top8f[:, 0:T], wtk[:, T:2 * T]))
            link(nc.vector.tensor_tensor(wtk[:, T:2 * T], wtk[:, 0:T], top8f[:, 0:T], ALU.mult))
            link(nc.vector.tensor_copy(wtk[:, 0:T], top8f[:, 0:T]))
            link(nc.vector.tensor_scalar(wtk, wtk, tg[:, 2:3], None, ALU.mult))
            v.wait_ge(s_rank, 1)
            c64 = cmp64.rearrange("p (e j) -> p e j", e=E_N)
            link(nc.vector.tensor_copy(tiles_c, psum[5][:, 64:64 + E_N]))
            link(nc.vector.tensor_tensor(c64, bc(tiles_c, T), c64, ALU.is_gt))
            link(nc.vector.tensor_reduce(tiles_e, c64, AX_X, ALU.add))
            link(nc.vector.tensor_tensor_scan(tiles_c, ones8, tiles_e, 0.0, ALU.mult, ALU.add))
            link(nc.vector.tensor_tensor(base_e, tiles_c, tiles_e, ALU.subtract))
            link(nc.vector.tensor_scalar(base_e, base_e, float(P), None, ALU.mult))
            se = slot_e.rearrange("p (t e) -> p t e", e=E_N)
            link(nc.vector.tensor_tensor(se, psum[5][:, 0:T * E_N].rearrange("p (t e) -> p t e", e=E_N),
                                         base_e.unsqueeze(1).to_broadcast([P, T, E_N]), ALU.add))
            pr = prod.rearrange("p (t k e) -> p t k e", t=T, k=TOPK)
            for k in range(TOPK):
                last = nc.vector.tensor_tensor(pr[:, :, k, :], oh[:, :, k, :], se, ALU.mult)
            link(last)
            link(nc.vector.tensor_reduce(slot_f, prod.rearrange("p (n e) -> p n e", e=E_N), AX_X, ALU.add))
            link(nc.vector.tensor_copy(slot_i, slot_f))
            nc.vector.tensor_scalar(tile_i, slot_i, 7, None, ALU.logical_shift_right)
            link(nc.vector.tensor_scalar(lane_i, slot_i, P - 1, None, ALU.bitwise_and))
            nc.vector.tensor_copy(tile_f, tile_i)
            link(nc.vector.tensor_copy(lane_f, lane_i))
            N2 = T * TOPK
            link(nc.vector.tensor_tensor(oh_lane, iota_lane[:, :].unsqueeze(1).to_broadcast([P, N2, P]), bc(lane_f, P), ALU.is_equal))
            link(nc.vector.tensor_tensor(oh_tile, tile_no.unsqueeze(1).to_broadcast([P, N2, NTP]), bc(tile_f, NTP), ALU.is_equal))
            nc.vector.tensor_scalar(ohv[:, :, 0, :], oh_tile, pcol[:, 0:1], None, ALU.mult)
            for t in range(T):
                last = nc.vector.tensor_scalar(ohv[:, TOPK * t:TOPK * (t + 1), 1, :], oh_tile[:, TOPK * t:TOPK * (t + 1), :], float(t), None, ALU.mult)
            last.then_inc(s_oh, 1)
            ev = cs[:, 0:NTP * E_N].rearrange("p (i e) -> p i e", e=E_N)
            v.wait_ge(s_oh, 1)
            link(nc.vector.tensor_tensor(ev, bc(tile_no, E_N), tiles_c.unsqueeze(1).to_broadcast([P, NTP, E_N]), ALU.is_ge))
            link(nc.vector.tensor_reduce(eid_f, ev, AX_X, ALU.add))
            link(nc.vector.tensor_scalar(eid_f, eid_f, float(E_N - 1), None, ALU.min))
            link(nc.vector.tensor_copy(eid_i, eid_f))
            v.wait_ge(s_tokp, 1)
            link(nc.vector.tensor_copy(eid_f, psum[6][:, 0:NTP]))
            link(nc.vector.scalar_tensor_tensor(tok_f, psum[6][:, NTP:2 * NTP], float(P), eid_f, ALU.mult, ALU.add))
            nc.vector.tensor_copy(tok_i, tok_f).then_inc(s_tab, 1)
            v.wait_ge(s_tab, 1)
            nc.vector.memset(ones8, 1.0).then_inc(s_free2, 1)

            def product(i):
                v.wait_ge(s_gs, i + 1)
                v.wait_ge(s_h3, i + 1)
                for h in range(2):
                    last = nc.vector.tensor_tensor(hm[:, h * MH:(h + 1) * MH], g_s[:, h * MH:(h + 1) * MH], psum[2 + h][:, 0:MH], ALU.mult)
                last.then_inc(s_hm, 1)

            def copy_hT(i):
                v.wait_ge(s_hTp, i + 1)
                nc.vector.tensor_copy(hT[:, 0:4, :], psum[4][:, :].rearrange("p (j s) -> p j s", s=P))
                nc.vector.tensor_copy(hT[:, 4:JF, :], psum[5][:, 0:(JF - 4) * P].rearrange("p (j s) -> p j s", s=P)).then_inc(s_hTs, 1)

            def copy_hT_later(i):
                v.wait_ge(s_y, i)
                copy_hT(i)

            product(0)
            copy_hT(0)
            product(1)
            copy_hT_later(1)
            product(2)
            with v.Fori(3, NT, 2) as i:
                copy_hT_later(i - 1)
                product(i)
                copy_hT_later(i)
                product(i + 1)
            copy_hT_later(NT - 1)

            v.wait_ge(s_yk, 16 * N2)
            for k in range(TOPK):
                for t in range(T):
                    last = nc.vector.scalar_tensor_tensor(X[:, t, :], yk[:, TOPK * t + k, :], wtk[:, k * T + t:k * T + t + 1],
                                                          X[:, t, :], ALU.mult, ALU.add)
                link(last)

            norm_stats(3)
            link(nc.vector.tensor_tensor(rms, rstd[:, :], rstd[:, :], ALU.mult))
            link(nc.vector.tensor_tensor(rms, rms, mv[:, :, 1], ALU.mult))
            nc.vector.tensor_scalar(rms, rms, RMS_EPS, None, ALU.add).then_inc(s_var, 1)
            v.wait_ge(s_std, 4)
            link(nc.vector.reciprocal(rms, rms))
            link(nc.vector.tensor_tensor(rstd[:, :], rstd[:, :], rms, ALU.mult))
            normalise(x3n).then_inc(s_x3n, 1)
            for n in range(4):
                part = slice(n * BANK, (n + 1) * BANK)
                v.wait_ge(s_qh, n + 1)
                link(nc.vector.scalar_tensor_tensor(q_rest[n % 2], psum[4 + n], ATT_SCALE, q_parts[:, 0, part], ALU.mult, ALU.subtract))
                link(nc.vector.tensor_copy(q_parts[:, 1, part], q_rest[n % 2]))
                nc.vector.tensor_tensor(q_parts[:, 2, part], q_rest[n % 2], q_parts[:, 1, part], ALU.subtract).then_inc(s_qp, 1)

            def max_unit(b, n):
                v.wait_ge(s_S, b * 16 + n + 1)
                lt, hp = n % TB, n // TB
                nc.vector.tensor_reduce(mx[:, lt, 2 * hp:2 * hp + 2], psum[n % 2].rearrange("p (g m) -> p g m", g=2), AX_X, ALU.max).then_inc(s_mx, 1)

            def max_parts(b):
                c = b * 4
                v.wait_ge(s_mx, b * 16 + 16)
                nc.vector.tensor_scalar(mneg, mx, -1.0, NO_KEY, ALU.mult, ALU.min).then_inc(chain, 1)
                v.wait_ge(chain, c + 1)
                nc.vector.tensor_copy(mparts[:, :, 0, :], mneg).then_inc(chain, 1)
                v.wait_ge(chain, c + 2)
                nc.vector.tensor_tensor(mneg, mneg, mparts[:, :, 0, :], ALU.subtract).then_inc(chain, 1)
                v.wait_ge(chain, c + 3)
                nc.vector.tensor_copy(mparts[:, :, 1, :], mneg).then_inc(chain, 1)
                v.wait_ge(chain, c + 4)
                nc.vector.tensor_tensor(mparts[:, :, 2, :], mneg, mparts[:, :, 1, :], ALU.subtract).then_inc(s_nm, 1)

            def max_copy(b):
                v.wait_ge(s_nmp, b + 1)
                if not isinstance(b, int) or b:
                    v.wait_ge(s_nmd, 48 * b)
                nc.vector.tensor_copy(mT[0:3 * NH, :], psbf[0][0:3 * NH, 0:S]).then_inc(s_nmc, 1)

            def normalise_chunk(b, c):
                v.wait_ge(s_PV, b * 8 + 2 * c + 2)
                if not isinstance(b, int) or b:
                    v.wait_ge(s_O, b)
                src = psum[6 + c % 2][:, 0:S]
                k = (b * 4 + c) * 2
                nc.vector.reciprocal(rec, src).then_inc(chain2, 1)
                v.wait_ge(chain2, k + 1)
                v.sem_inc(s_alone, 1)
                nc.vector.stream_shuffle(rec_s, rec, [HD + i % HD for i in range(32)]).then_inc(chain2, 1)
                v.wait_ge(chain2, k + 2)
                nc.vector.scalar_tensor_tensor(attn[:, c, :], rec_s, -MASKED, src, ALU.min, ALU.mult).then_inc(s_at, 1)

            def add_out(b):
                v.wait_ge(s_O, b + 1)
                xb = X[:, bass.ds(b * TB, TB), :].rearrange("p t d -> p (t d)")
                nc.vector.tensor_tensor(o_tmp, psum[7], gate_s[:, bass.ds(b * TB * D, TB * D)], ALU.mult).then_inc(chain3, 1)
                v.wait_ge(chain3, b + 1)
                nc.vector.tensor_tensor(xb, xb, o_tmp, ALU.add).then_inc(s_oe, 1)

            def attention(b, ahead=True):
                for hp in range(8):
                    if ahead:
                        max_unit(b + 1, 2 * hp)
                        max_unit(b + 1, 2 * hp + 1)
                    if hp in (2, 4, 6):
                        normalise_chunk(b, hp // 2 - 1)
                if ahead:
                    max_parts(b + 1)
                normalise_chunk(b, 3)
                if ahead:
                    max_copy(b + 1)
                add_out(b)

            for n in range(16):
                max_unit(0, n)
            max_parts(0)
            max_copy(0)
            v.wait_ge(s_gsc, 1)
            attention(0)
            with v.Fori(1, B - 1) as b:
                attention(b)
            attention(B - 1, False)

            v.wait_ge(s_oe, B)
            norm_stats(5)

            def norm_tile(t, u):
                if not isinstance(t, int) or t >= 2:
                    v.wait_ge(s_fT, t - 1)
                nc.vector.tensor_scalar(x4n[u], X[:, bass.ds(t, 1), :].rearrange("p t d -> p (t d)"), mean_of(t), rstd[:, bass.ds(t, 1)],
                                        ALU.subtract, ALU.mult).then_inc(s_xf, 1)

            def mean_of(t):
                return mv[:, bass.ds(t, 1), 0:1].rearrange("p t o -> p (t o)")

            FS = 9

            def route(t, u):
                k = [0]

                def step(ins):
                    k[0] += 1
                    ins.then_inc(chain4, 1)
                    v.wait_ge(chain4, t * FS + k[0])
                    v.sem_inc(s_alone, 1)

                v.wait_ge(s_sq, t + 1)
                nc.vector.tensor_reduce(norm2, vecs2.rearrange("p (a r) -> p a r", r=NR), AX_X, ALU.add).then_inc(s_ar, 1)
                v.wait_ge(s_ar, t + 1)
                v.sem_inc(s_alone, 1)
                step(nc.vector.max(f_top, norm2))
                step(nc.vector.max_index(f_topi, f_top, norm2))
                step(nc.vector.tensor_copy(f_topf, f_topi))
                step(nc.vector.tensor_scalar(routes, iota_lane[:, 0:NA], f_topf[:, 0:1], None, ALU.is_equal))
                for j in range(1, RTOP):
                    step(nc.vector.scalar_tensor_tensor(routes, iota_lane[:, 0:NA], f_topf[:, j:j + 1], routes, ALU.is_equal, ALU.add))
                vec = PS[:, 2 * u * BANK:(2 * u + 2) * BANK]
                nc.vector.tensor_tensor(picked.rearrange("p (a r) -> p a r", r=NR), vec.rearrange("p (a r) -> p a r", r=NR),
                                        bc(routes, NR), ALU.mult).then_inc(s_pk, 1)
                v.wait_ge(s_pk, t + 1)
                step(nc.vector.tensor_reduce(v_sum, picked.rearrange("p (a r) -> p r a", r=NR), AX_X, ALU.add))
                step(nc.vector.tensor_scalar(v_sum, v_sum, 1.0 / RTOP ** 2, None, ALU.mult))
                if not isinstance(t, int) or t:
                    v.wait_ge(s_uT, t)
                nc.vector.tensor_tensor(u_s.rearrange("p (a r) -> p a r", r=NR), bc(routes, NR),
                                        v_sum.unsqueeze(1).to_broadcast([P, NA, NR]), ALU.mult).then_inc(s_u, 1)
                assert k[0] == FS

            def final(t):
                v.wait_ge(s_D, t + 1)
                xt = X[:, bass.ds(t, 1), :].rearrange("p t d -> p (t d)")
                nc.vector.scalar_tensor_tensor(xt, psum[6][:, 0:D], tg[:, 3:4], xt, ALU.mult, ALU.add).then_inc(s_fin, 1)

            def maps(t, u, ahead=2):
                route(t, u)
                if ahead >= 2:
                    norm_tile(t + 2, u)
                if not isinstance(t, int) or t:
                    final(t - 1)

            norm_tile(0, 0)
            norm_tile(1, 1)
            maps(0, 0)
            with v.Fori(1, T - 3, 2) as t:
                maps(t, 1)
                maps(t + 1, 0)
            maps(T - 3, 1)
            maps(T - 2, 0, 1)
            maps(T - 1, 1, 0)
            final(T - 1)

        @block.tensor
        def _(pe):
            pe.wait_ge(s_const, 1)
            pe.wait_ge(s_kvw, 32)
            for n in range(2):
                for k in range(KD):
                    for c in range(KD):
                        last = nc.tensor.transpose(psum[n][:, k * D + c * P:k * D + (c + 1) * P], kv_raw[:, n, c, k * P:(k + 1) * P], ident[:, :])
            last.then_inc(s_kvT, 1)
            pe.wait_ge(s_c, 16)
            for n in range(4):
                for t in range(4):
                    tt = (n % 2) * 4 + t
                    last = nc.tensor.transpose(psum[2 + n][:, t * P:(t + 1) * P], ctx_rows[:, tt * D + (n // 2) * P:tt * D + (n // 2 + 1) * P], ident[:, :])
            last.then_inc(s_kvT, 1)
            pe.wait_ge(s_kvTc, 6)
            for n, bank in enumerate((0, 1, 6, 7)):
                c, h = n // 2, n % 2
                for k in range(KD):
                    last = nc.tensor.matmul(psum[bank], kv_wT[:, 0, k, c * P:(c + 1) * P], ctxT[:, k, h * BANK:(h + 1) * BANK],
                                            start=(k == 0), stop=(k == KD - 1))
                last.then_inc(s_kv, 1)
            for t in range(T):
                for k in range(KD):
                    last = nc.tensor.matmul(psum[2 + t // 2][:, (t % 2) * D:(t % 2 + 1) * D], ctxT[:, k, t * P:(t + 1) * P], kv_wT[:, 1, k, :],
                                            start=(k == 0), stop=(k == KD - 1))
                if t % 2:
                    last.then_inc(s_kv, 1)
            pe.wait_ge(s_kvc, 8)

            for g, (src, ready) in enumerate(((qc_bf, s_qc), (qx_bf, s_qx))):
                pe.wait_ge(ready, 1)
                for k in range(KD):
                    for t in range(T):
                        last = nc.tensor.transpose(psbf[4 * g + k][:, t * P:(t + 1) * P], src[:, t * D + k * P:t * D + (k + 1) * P], ident_bf[:, :])
                last.then_inc(s_tr, 2)
            pe.wait_ge(s_trc, 2 * KD)
            for t in range(T):
                b = t // TB
                for k in range(KD):
                    last = nc.tensor.matmul(psum[t][:, k * D:(k + 1) * D], qxT[:, k, t * P:(t + 1) * P],
                                            qcT[:, k, b * S:(b + 1) * S], start=True, stop=True)
                last.then_inc(s_xa, 1)
            pe.wait_ge(s_xn2, 1)
            for n in range(4):
                for t in range(4):
                    tt = (n % 2) * 4 + t
                    last = nc.tensor.transpose(psum[n][:, t * P:(t + 1) * P], xn[:, tt * D + (n // 2) * P:tt * D + (n // 2 + 1) * P], ident[:, :])
                last.then_inc(s_x2T, 1)
            pe.wait_ge(s_gw, 16)
            pe.wait_ge(s_x2Tc, 4)
            for t in range(T):
                for k in range(KD):
                    last = nc.tensor.matmul(psum[4][:, t * E_N:(t + 1) * E_N], xnT[:, k, t * P:(t + 1) * P], gate_w[:, k, :],
                                            start=(k == 0), stop=(k == KD - 1))
            last.then_inc(s_rt, 1)
            pe.wait_ge(s_hits, 1)
            hb = hits_bf.rearrange("p (t e) -> p t e", e=E_N)
            rank = psum[5][:, 0:T * E_N].rearrange("p (t e) -> p t e", e=E_N)
            nc.tensor.matmul(rank, before_bf[:, :], hb, start=True, stop=False, skip_group_check=True)
            for t in range(T - 1):
                nc.tensor.matmul(rank[:, t + 1:T, :], ones_bf[:, :], hb[:, t:t + 1, :].to_broadcast([P, T - 1 - t, E_N]),
                                 start=False, stop=(t == T - 2), skip_group_check=True)
            for t in range(T):
                last = nc.tensor.matmul(psum[5][:, 64:64 + E_N], ones_bf[:, :], hb[:, t, :], start=False, stop=(t == T - 1), skip_group_check=True)
            last.then_inc(s_rank, 1)
            pe.wait_ge(s_oh, 1)
            for n in range(T * TOPK):
                last = nc.tensor.matmul(psum[6][:, 0:2 * NTP], oh_lane[:, n, :], ohv[:, n, :, :].rearrange("p a b -> p (a b)"),
                                        start=(n == 0), stop=(n == T * TOPK - 1))
            last.then_inc(s_tokp, 1)

            pe.wait_ge(s_tab, 1)

            def expert(i):
                return pe.value_load(eid_i[0:1, bass.ds(i, 1)], min_val=0, max_val=E_N - 1)

            def transpose_x(i, u, landed):
                pe.wait_ge(s_rows[u], 16 * landed)
                for k in range(KD):
                    last = nc.tensor.transpose(psum[6][:, k * P:(k + 1) * P], xg[u][:, k * P:(k + 1) * P], ident[:, :])
                last.then_inc(s_xTp, 1)

            def up(i, u, e, n):
                for h in range(2):
                    for k in range(KD):
                        last = nc.tensor.matmul(psum[2 * n + h][:, 0:MH], xgT[u][:, k, :],
                                                W[:, bass.ds(e * WE + (n * KD + k) * M_F + h * MH, MH)],
                                                start=(k == 0), stop=(k == KD - 1))
                last.then_inc((s_h1, s_h3)[n], 1)

            def transpose_h(i):
                for j in range(JF):
                    last = nc.tensor.transpose(psum[4 + j // 4][:, (j % 4) * P:(j % 4 + 1) * P], hm[:, j * P:(j + 1) * P], ident[:, :])
                last.then_inc(s_hTp, 1)

            def down(i, e):
                pe.wait_ge(s_hTs, i + 1)
                for j in range(JF):
                    last = nc.tensor.matmul(psum[7][:, 0:D], hT[:, j, :], W[:, bass.ds(e * WE + 2 * KD * M_F + j * D, D)],
                                            start=(j == 0), stop=(j == JF - 1))
                last.then_inc(s_y, 1)

            def tile(i, u, landed_next, last_tile=False, first_y=False):
                e = expert(i)
                pe.wait_ge(s_xTs, i + 1)
                pe.wait_ge(s_wr, e + 1)
                pe.wait_ge(s_gs, i)
                up(i, u, e, 0)
                pe.wait_ge(s_hm, i)
                transpose_h(i - 1)
                up(i, u, e, 1)
                if not last_tile:
                    transpose_x(i + 1, 1 - u, landed_next)
                e0 = expert(i - 1)
                if not first_y:
                    pe.wait_ge(s_ys, i - 1)
                down(i - 1, e0)

            transpose_x(0, 0, 1)
            e = expert(0)
            pe.wait_ge(s_xTs, 1)
            pe.wait_ge(s_wr, e + 1)
            up(0, 0, e, 0)
            up(0, 0, e, 1)
            transpose_x(1, 1, 1)
            tile(1, 1, 2, first_y=True)
            tile(2, 0, 2)
            with pe.Fori(3, NT - 2, 2) as i:
                half = pe.snap(i // 2)
                tile(i, 1, half + 2)
                tile(i + 1, 0, half + 2)
            tile(NT - 2, 1, (NT - 1) // 2 + 1)
            tile(NT - 1, 0, 0, last_tile=True)
            pe.wait_ge(s_hm, NT)
            transpose_h(NT - 1)
            e = expert(NT - 1)
            pe.wait_ge(s_ys, NT - 1)
            down(NT - 1, e)

            pe.wait_ge(s_prew, 48)
            for n in range(2):
                for k in range(KD):
                    for c in range(KD):
                        last = nc.tensor.transpose(psum[n][:, k * D + c * P:k * D + (c + 1) * P], l1_raw[:, n, c, k * P:(k + 1) * P], ident[:, :])
            last.then_inc(s_l1T, 1)
            pe.wait_ge(s_wop, 1)
            for c in range(NC):
                for o in range(KD):
                    last = nc.tensor.transpose(psum[2 + c // 2][:, (c % 2) * D + o * P:(c % 2) * D + (o + 1) * P],
                                               wo_wide[:, o, c * HC:(c + 1) * HC, :].rearrange("p h w -> p (h w)"), ident[:, :])
            last.then_inc(s_l1T, 1)
            pe.wait_ge(s_ffw, 64)
            pe.wait_ge(s_ys, NT)
            for n in range(4):
                for j in range(4):
                    jj = (n % 2) * 4 + j
                    last = nc.tensor.transpose(psum[4 + n][:, j * P:(j + 1) * P], a_raw[:, jj, (n // 2) * P:(n // 2 + 1) * P], ident[:, :])
            last.then_inc(s_l1T, 1)
            pe.wait_ge(s_l1Tc, 8)
            for j in range(JA):
                for o in range(KD):
                    nc.tensor.transpose(psum[4 + j // 2][:, (j % 2) * D + o * P:(j % 2) * D + (o + 1) * P], b_raw[:, o, j * P:(j + 1) * P], ident[:, :])
            for k in range(KD):
                for o in range(KD):
                    last = nc.tensor.transpose(psum[0][:, k * D + o * P:k * D + (o + 1) * P], w_raw[:, o, k * P:(k + 1) * P], ident[:, :])
            last.then_inc(s_l1T, 1)
            pe.wait_ge(s_x3n, 1)
            pe.wait_ge(s_l1Tc, 13)
            for n in range(4):
                for t in range(4):
                    tt = (n % 2) * 4 + t
                    last = nc.tensor.transpose(psum[n][:, t * P:(t + 1) * P], x3n[:, tt * D + (n // 2) * P:tt * D + (n // 2 + 1) * P], ident[:, :])
                last.then_inc(s_x3T, 1)
            pe.wait_ge(s_x3Tc, 4)
            for n in range(4):
                c, h = n // 2, n % 2
                for k in range(KD):
                    last = nc.tensor.matmul(psum[4 + n], qg_wT[:, 0, k, c * P:(c + 1) * P], x3T[:, k, h * BANK:(h + 1) * BANK],
                                            start=(k == 0), stop=(k == KD - 1))
                last.then_inc(s_q, 1)
            for t in range(T):
                for k in range(KD):
                    last = nc.tensor.matmul(psum[t // 2][:, (t % 2) * D:(t % 2 + 1) * D], x3T[:, k, t * P:(t + 1) * P], qg_wT[:, 1, k, :],
                                            start=(k == 0), stop=(k == KD - 1))
                if t % 2:
                    last.then_inc(s_gt, 1)

            def scores(b, n):
                g = b * 16 + n
                lt, hp = n % TB, n // TB
                if not isinstance(g, int) or g >= 2:
                    pe.wait_ge(s_mx, g - 1)
                if n == 0 and (not isinstance(b, int) or b):
                    pe.wait_ge(s_nmc, b)
                for i in range(2):
                    h = 2 * hp + i
                    last = nc.tensor.matmul(psum[n % 2][:, i * S:(i + 1) * S], Qp[0:ROWS_S, h, bass.ds(b * S + lt * P, P)],
                                            Kp[0:ROWS_S, h, bass.ds(b * S, S)], start=True, stop=True)
                last.then_inc(s_S, 1)

            def max_transposes(b):
                pe.wait_ge(s_nm, b + 1)
                pe.sem_inc(s_alone, 1)
                for lt in range(TB):
                    last = nc.tensor.transpose(psbf[0][0:3 * NH, lt * P:(lt + 1) * P], mparts[:, lt, :, :].rearrange("p j h -> p (j h)"), ident_bf[:, :])
                last.then_inc(s_nmp, 1)

            def scores_T(b, hp):
                g = b * 8 + hp
                if not isinstance(g, int) or g >= 2:
                    pe.wait_ge(s_pt, g - 1)
                for i in range(2):
                    h = 2 * hp + i
                    for m in range(TB):
                        last = nc.tensor.matmul(psum[2 + 2 * (hp % 2) + i][:, m * S:(m + 1) * S], Kp[0:ROWS_ST, h, bass.ds(b * S + m * P, P)],
                                                Qp[0:ROWS_ST, h, bass.ds(b * S, S)], start=True, stop=True)
                last.then_inc(s_ST, 1)

            def pv(b, hp):
                g = b * 8 + hp
                c = hp // 2
                pe.wait_ge(s_pt, g + 1)
                if hp == 0:
                    pe.wait_ge(s_vw, b + 1)
                if hp % 2 == 0 and (not isinstance(b, int) or b * 4 + c >= 2):
                    pe.wait_ge(s_at, b * 4 + c - 1)
                if hp == 2 and (not isinstance(b, int) or b):
                    pe.wait_ge(s_oe, b)
                for i in range(2):
                    h = 2 * hp + i
                    r = 32 * (h % HC)
                    for m in range(TB):
                        last = nc.tensor.matmul(psum[6 + c % 2][r:r + 32, 0:S], v_wide[:, m, h, :],
                                                probs[hp % 2][:, i, m, :], start=(m == 0), stop=(m == TB - 1))
                last.then_inc(s_PV, 1)

            def out_product(b):
                pe.wait_ge(s_at, b * 4 + 4)
                if not isinstance(b, int) or b:
                    pe.wait_ge(s_oe, b)
                for lt in range(TB):
                    for c in range(NC):
                        last = nc.tensor.matmul(psum[7][:, lt * D:(lt + 1) * D], attn[:, c, lt * P:(lt + 1) * P], wo_wT[:, c, :],
                                                start=(c == 0), stop=(c == NC - 1))
                last.then_inc(s_O, 1)

            def attention(b, ahead=True):
                pe.wait_ge(s_nmd, 48 * (b + 1))
                for hp in range(8):
                    if ahead:
                        scores(b + 1, 2 * hp)
                        scores(b + 1, 2 * hp + 1)
                    scores_T(b, hp)
                    if hp:
                        pv(b, hp - 1)
                pv(b, 7)
                if ahead:
                    max_transposes(b + 1)
                out_product(b)

            pe.wait_ge(s_kp, 16 * 11)
            pe.wait_ge(s_qpk, 16 * 6)
            pe.wait_ge(s_gtc, 4)
            pe.wait_ge(s_qp, 4)
            for n in range(16):
                scores(0, n)
            max_transposes(0)
            attention(0)
            with pe.Fori(1, B - 1) as b:
                attention(b)
            attention(B - 1, False)

            def transpose_x4(t, u):
                pe.wait_ge(s_xf, t + 1)
                if isinstance(t, int) and t == 0:
                    pe.wait_ge(s_oe, B)
                else:
                    pe.wait_ge(s_fTc, t)
                for k in range(KD):
                    last = nc.tensor.transpose(psum[7][:, k * P:(k + 1) * P], x4n[u][:, k * P:(k + 1) * P], ident[:, :])
                last.then_inc(s_fT, 1)

            def vectors(t, u):
                pe.wait_ge(s_fTc, t + 1)
                if not isinstance(t, int) or t >= 2:
                    pe.wait_ge(s_pk, t - 1)
                for h in range(2):
                    for k in range(KD):
                        last = nc.tensor.matmul(psum[2 * u + h], x4T[u][:, k, :], aT[:, k, h * BANK:(h + 1) * BANK],
                                                start=(k == 0), stop=(k == KD - 1))
                last.then_inc(s_V, 1)

            def transpose_u(t):
                pe.wait_ge(s_u, t + 1)
                for j in range(JA):
                    last = nc.tensor.transpose(psum[4 + j // 4][:, (j % 4) * P:(j % 4 + 1) * P], u_s[:, j * P:(j + 1) * P], ident[:, :])
                last.then_inc(s_uT, 1)

            def base_and_delta(t, u):
                if not isinstance(t, int) or t:
                    pe.wait_ge(s_fin, t)
                nc.tensor.matmul(psum[6][:, 0:D], ones_row[0:1, :], bias_row[0:1, :], start=True, stop=False)
                for k in range(KD):
                    nc.tensor.matmul(psum[6][:, 0:D], x4T[u][:, k, :], wT[:, k, :], start=False, stop=False)
                pe.wait_ge(s_uTc, t + 1)
                for j in range(JA):
                    last = nc.tensor.matmul(psum[6][:, 0:D], uT[:, j, :], bT[:, j, :], start=False, stop=(j == JA - 1))
                last.then_inc(s_D, 1)

            def maps(t, u, ahead=2):
                if ahead >= 1:
                    vectors(t + 1, 1 - u)
                transpose_u(t)
                base_and_delta(t, u)
                if ahead >= 2:
                    transpose_x4(t + 2, u)

            transpose_x4(0, 0)
            vectors(0, 0)
            transpose_x4(1, 1)
            maps(0, 0)
            with pe.Fori(1, T - 3, 2) as t:
                maps(t, 1)
                maps(t + 1, 0)
            maps(T - 3, 1)
            maps(T - 2, 0, 1)
            maps(T - 1, 1, 0)


_INS = ["x", "ctx_2048", "mask_BxS2_bk0", "g_xattn", "g_ffn", "L0_ffn_gate_w", "L0_ffn_w1", "L0_ffn_w2", "L0_ffn_w3",
        "L1_xattn_norm_w", "L1_xattn_wq", "L1_xattn_wk", "L1_xattn_wv", "L1_xattn_wo", "L1_xattn_wg",
        "L1_ffn_A", "L1_ffn_B", "L1_ffn_W", "L1_ffn_bias"]


def kernel(**inputs):
    import numpy as _np
    import concourse.bacc as _bacc
    from concourse import mybir as _mybir
    from concourse.bass_utils import run_bass_kernel_spmd as _run

    nc = _bacc.Bacc("TRN2", target_bir_lowering=False, num_devices=1)
    arrays, aps = {}, {}
    for name in _INS:
        x = _np.ascontiguousarray(inputs[name])
        arrays[f"in_{name}_dram"] = x
        aps[name] = nc.dram_tensor(f"in_{name}_dram", x.shape, _mybir.dt.from_np(x.dtype), kind="ExternalInput").ap()
    aps["out"] = nc.dram_tensor("out_dram", (B, S, D), _mybir.dt.float32, kind="ExternalOutput").ap()
    flamingo(nc, aps)
    r = _run(nc, [arrays], core_ids=[0])
    return r.results[0]["out_dram"]
```

```python
from contextlib import ExitStack

import concourse.bass as bass
from concourse import mybir
from concourse.alu_op_type import AluOpType as ALU

ACT = mybir.ActivationFunctionType
F32 = mybir.dt.float32
F32R = mybir.dt.float32r
BF16 = mybir.dt.bfloat16
I32 = mybir.dt.int32
U32 = mybir.dt.uint32
U8 = mybir.dt.uint8
AX_X = mybir.AxisListType.X
RMAX = bass.bass_isa.ReduceOp.max

P = 128
B, S, D = 4, 256, 256
T = B * S // P
TB = S // P
KD = D // P
FP8_MAX, ACT_EPS, W_EPS = 448.0, 1e-4, 1e-6
LN_EPS, RMS_EPS = 1e-5, 1e-6

E_N, M_F, TOPK = 8, 896, 2
MH = M_F // 2
JF = M_F // P
NT = (B * S * TOPK - E_N) // P + E_N
NT_MIN = B * S * TOPK // P
NTP = NT + 1
TABS = 6
UNITS = [([0, 1], [2, 3]), ([4, 5], []), ([6, 7], []), ([8, 9, 10], []), ([11, 12], [13, 14, 15]), ([], []), ([], []), ([], [])]
LAST_UNITS = 4
EARLY, REST = range(T // 2), range(T // 2, T)
FIRST, OTHERS = range(TB), range(TB, T)
CHUNKS = [range(0, 2), range(2, 4), range(4, 8)]
X2_BANK = [6, 2]
X3_BANK, Q_BANK = [0, 2, 0], [4, 6, 2]
WE = 2 * KD * M_F + JF * D
LATE = 4

BANK = 512

NH, HD = 16, 16
ATT_SCALE = HD ** -0.5
HC = 4
NC = NH // HC
Q_PART = (0, 0, 1, 1, 0, 2)
K_PART = (0, 1, 0, 1, 2, 0)
ROWS_QK = 6 * HD
ROWS_S, ROWS_ST = ROWS_QK + 1, ROWS_QK + 4
MASKED, NO_KEY = -1e30, 1e29

NA, NR, RTOP = 64, 16, 4
AR = NA * NR
JA = AR // P


def bc(ap, n):
    return ap.unsqueeze(2).to_broadcast([ap.shape[0], ap.shape[1], n])


def flamingo(nc, a):
    out = a["out"]
    ctx = ExitStack()
    with ctx:
        def sb(name, shape, dt=F32):
            return ctx.enter_context(nc.sbuf_tensor(name, shape, dt))

        def sem(name):
            return ctx.enter_context(nc.semaphore(name))

        def dram(name, shape, dt=F32):
            return nc.dram_tensor(name, shape, dt, kind="Internal").ap()

        X = sb("X", [P, T, D])
        W_at = nc.sbuf_base
        W = sb("W", [P, E_N * WE])
        SCR_at = nc.sbuf_base
        SCR = sb("SCR", [P, 4608])
        assert SCR_at == W_at + 4 * E_N * WE and nc.sbuf_base == SCR_at + 4 * 4608

        def float32r(name, at, n):
            return nc.alloc_sbuf_tensor_at(name, [P, n], F32R, offset=W_at + 4 * at)

        ident = sb("ident", [P, P])
        ident_bf = sb("ident_bf", [P, P], BF16)
        ones_bf = sb("ones_bf", [P, P], BF16)
        before_bf = sb("before_bf", [P, P], BF16)
        iota_lane = sb("iota_lane", [P, P])
        pcol = sb("pcol", [P, 1])
        sum_cols = sb("sum_cols", [P, NC * NH + 4 * HC])
        eps_ln = sb("eps_ln", [P, 1])
        gates = sb("gates", [P, 4])
        tg = sb("tg", [P, 4])
        stats = sb("stats", [P, T, 6])
        mv = sb("mv", [P, T, 2])
        rstd = sb("rstd", [P, T])
        SM = sb("SM", [P, 2620])

        PS = ctx.enter_context(nc.psum_tensor("PS", [P, 8 * BANK], F32))
        psum = [PS[:, i * BANK:(i + 1) * BANK] for i in range(8)]
        psbf = [x.bitcast(BF16) for x in psum]

        at = [0]

        def small(n):
            at[0] += n
            assert at[0] <= SM.shape[1]
            return SM[:, at[0] - n:at[0]]

        NB = T * KD
        amax_x, amax_c, amax_ca = small(NB), small(NB), small(NB)
        qs_x, qs_c, ds_x, ds_c = small(NB), small(NB), small(NB), small(NB)
        coef = small(T * KD * TB).rearrange("p (t k n) -> p t k n", t=T, k=KD)
        logits_v = small(T * E_N)
        top8 = small(T * 8)
        top8i = small(T * 8).bitcast(U32)
        top8f = small(T * 8)
        onehot = small(T * TOPK * E_N)
        hits_bf = small(T * E_N // 2).bitcast(BF16)
        wtk = small(T * TOPK)
        tiles_e, tiles_c, base_e, ones8 = small(E_N), small(E_N), small(E_N), small(E_N)
        cmp64 = small(64)
        slot_e = small(T * E_N)
        prod = small(T * TOPK * E_N)
        slot_f = small(T * TOPK)
        slot_i, lane_i, tile_i = (small(T * TOPK).bitcast(I32) for _ in range(3))
        count_i = small(1).bitcast(I32)
        tile_no = small(NTP)
        tok_f, tok_i, sc_f, sc_i = small(NTP), small(NTP).bitcast(I32), small(NTP), small(NTP).bitcast(I32)
        eid_f, eid_i = small(NTP), small(NTP).bitcast(I32)
        last_i = small(1).bitcast(I32)
        slot_gate, filled = small(NTP), small(NTP)
        dummy_row = small(1)
        gate_rest = small(T * TOPK)
        values = small(T * TOPK * TABS // 2).bitcast(BF16).rearrange("p (n a) -> p n a", a=TABS)
        lane_no_bf, tile_no_bf = small(P // 2).bitcast(BF16), small(NTP // 2).bitcast(BF16)
        choice_tile = small(T * TOPK)
        lane_bf, tile_bf = small(T * TOPK // 2).bitcast(BF16), small(T * TOPK // 2).bitcast(BF16)
        idx_col, sc_col = small(2).bitcast(I32), small(2).bitcast(I32)

        def wt(e):
            return W[:, e * WE:(e + 1) * WE]

        late = [(E_N - LATE) * WE]

        def early(n):
            late[0] += n
            assert late[0] <= E_N * WE
            return W[:, late[0] - n:late[0]]

        ctx_rows, xn, xs, mag, cs = (early(T * D) for _ in range(5))
        kv_raw = early(2 * KD * D).rearrange("p (w t d) -> p w t d", w=2, t=KD)
        kv_wT = early(2 * KD * D).rearrange("p (w k c) -> p w k c", w=2, k=KD)
        ctxT = early(KD * B * S).rearrange("p (k t) -> p k t", k=KD)
        k32 = early(KD * B * S)
        k_parts = early(3 * KD * B * S // 2).bitcast(BF16).rearrange("p (j n) -> p j n", j=3)
        v32 = early(T * D)
        post = [0]

        def room(n):
            post[0] += n
            assert post[0] <= E_N * WE
            return W[:, post[0] - n:post[0]]

        def room_r(name, n):
            room(n)
            return float32r(name, post[0] - n, n)

        q_parts_room = room(3 * KD * B * S // 2)
        q_parts = q_parts_room.bitcast(BF16).rearrange("p (j n) -> p j n", j=3)
        l1_raw_room = room(3 * KD * D)
        x4_r = float32r("x4T_parts", post[0] - 4 * D, 4 * D)
        l1_raw = l1_raw_room.rearrange("p (w t d) -> p w t d", w=3, t=KD)
        wo_wide_room = room(KD * NH * 32)
        wo_wide = wo_wide_room.rearrange("p (t h w) -> p t h w", t=KD, h=NH)
        qg_wT = room(2 * KD * D).rearrange("p (w k c) -> p w k c", w=2, k=KD)
        wo_wT = room(NC * D).rearrange("p (c n) -> p c n", c=NC)
        f_at = post[0]
        Qp = room(NH * B * S // 2).bitcast(BF16).rearrange("p (h t) -> p h t", h=NH)
        Kp = room(NH * B * S // 2).bitcast(BF16).rearrange("p (h t) -> p h t", h=NH)
        v_wide = room(TB * NH * 32).rearrange("p (m h w) -> p m h w", m=TB, h=NH)
        v_rows = room(T * D)
        bT_lo = float32r("bT_low", post[0] - T * D, T * D).rearrange("p (j d) -> p j d", j=JA)
        probs_w = room(3 * 1024)
        wT_lo = float32r("wT_low", post[0] - 1024, KD * D).rearrange("p (k n) -> p k n", k=KD)
        probs = [probs_w[:, i * 1024:(i + 1) * 1024].rearrange("p (g m l) -> p g m l", g=2, m=TB) for i in range(2)]
        q_rest = [probs_w[:, 2048 + i * BANK:2048 + (i + 1) * BANK] for i in range(2)]
        gate_s = room(T * D)
        misc_room = room_r("bias_parts", 2 * D + P)
        inv_raw, inv = room(S), room(S)
        spread = room(NC * P).rearrange("p (c m) -> p c m", c=NC)
        o_tmp = room(TB * D)
        a_raw = room(JA * D).rearrange("p (j d) -> p j d", j=JA)
        b_raw = q_parts_room[:, 0:KD * AR].rearrange("p (j n) -> p j n", j=KD)
        w_raw = room(KD * D).rearrange("p (t d) -> p t d", t=KD)
        aT = room_r("aT_high", KD * AR).rearrange("p (k n) -> p k n", k=KD)
        bT = room_r("bT_high", JA * D).rearrange("p (j d) -> p j d", j=JA)
        wT = room_r("wT_high", KD * D).rearrange("p (k n) -> p k n", k=KD)
        x3n = SCR[:, 0:T * D]
        attn = [SCR[:, i * NC * S:(i + 1) * NC * S].rearrange("p (c l) -> p c l", c=NC) for i in range(2)]
        assert 2 * NC * S <= T * D
        x3T = SCR[:, T * D:2 * T * D].rearrange("p (k t) -> p k t", k=KD)
        def f_room(at, n):
            return Qp.rearrange("p h t -> p (h t)").bitcast(F32)[:, at:at + n]

        x4n = [l1_raw_room[:, i * D:(i + 1) * D] for i in range(2)]
        x4T, x4T_lo = ([x4_r[:, (2 * n + i) * D:(2 * n + i + 1) * D].rearrange("p (k s) -> p k s", k=KD) for i in range(2)]
                       for n in range(2))
        x4T_whole = [wo_wide_room[:, i * D:(i + 1) * D].rearrange("p (k s) -> p k s", k=KD) for i in range(2)]
        vecs2, picked, u_s, uT_whole_flat = (f_room((1 + i) * AR, AR) for i in range(4))
        uT_flat, uT_lo_flat = (float32r(name, f_at + i * AR, AR) for name, i in (("uT_high", 5), ("uT_low", 6)))
        uT, uT_whole, uT_lo = (x.rearrange("p (j s) -> p j s", j=JA) for x in (uT_flat, uT_whole_flat, uT_lo_flat))
        norm2 = f_room(7 * AR, NA)
        f_top, f_topi, f_topf = f_room(7 * AR + 64, 8), f_room(7 * AR + 72, 8).bitcast(U32), f_room(7 * AR + 80, 8)
        routes = [f_room(7 * AR + 96 + i * NA, NA) for i in range(2)]
        v_sum = [f_room(7 * AR + 224 + i * NR, NR) for i in range(2)]
        is_top = f_room(7 * AR + 256, NA * RTOP)
        aT_lo = float32r("aT_low", E_N * WE + T * D, KD * AR).rearrange("p (k n) -> p k n", k=KD)
        bias_parts, ones_part = misc_room[:, 0:2 * D], misc_room[:, 2 * D:2 * D + P]
        assert AR == B * S and 7 * AR + 256 + NA * RTOP <= NH * B * S // 2
        prep_src = [[a_raw[:, (n % 2) * 4 + j, (n // 2) * P:(n // 2 + 1) * P] for j in range(4)] for n in range(4)]
        prep_dst = [aT[:, n // 2, (n % 2) * BANK:(n % 2 + 1) * BANK] for n in range(4)]
        prep_lo = [aT_lo[:, n // 2, (n % 2) * BANK:(n % 2 + 1) * BANK] for n in range(4)]
        prep_src.append([w_raw[:, o, k * P:(k + 1) * P] for k in range(KD) for o in range(KD)])
        prep_dst.append(wT.rearrange("p k n -> p (k n)"))
        prep_src += [[b_raw[:, o, j * P:(j + 1) * P] for j in (2 * n, 2 * n + 1) for o in range(KD)] for n in range(JA // 2)]
        prep_lo.append(wT_lo.rearrange("p k n -> p (k n)"))
        prep_lo += [bT_lo[:, 2 * n:2 * n + 2, :].rearrange("p j d -> p (j d)") for n in range(JA // 2)]
        prep_scale = [1.0] * 5 + [1.0 / RTOP ** 2] * 4
        prep_dst += [bT[:, 2 * n:2 * n + 2, :].rearrange("p j d -> p (j d)") for n in range(JA // 2)]
        nw = small(KD)
        rms = small(T)
        root_spare = small(1)
        mx = small(TB * NH).rearrange("p (t h) -> p t h", t=TB)
        mneg = small(TB * NH).rearrange("p (t h) -> p t h", t=TB)
        mparts = small(TB * 3 * NH // 2).bitcast(BF16).rearrange("p (t j h) -> p t j h", t=TB, j=3)
        mT = small(S // 2).bitcast(BF16)
        bias_row = small(D)
        mask_u8 = small(B * S // 4).bitcast(U8)[0:1, :]
        mag_c = v32
        kv_raw_flat = kv_raw.rearrange("p w t d -> p (w t d)")
        mask_row = kv_raw_flat[0:1, 0:B * S // 2].bitcast(BF16)
        one_row = kv_raw_flat[0:1, B * S // 2:B * S].bitcast(BF16)
        ones_row = small(P)
        qx_bf = SCR[:, 0:1024].bitcast(BF16)
        qc_bf = SCR[:, 1024:2048].bitcast(BF16)
        qxT = SCR[:, 2048:3072].bitcast(BF16).rearrange("p (k t) -> p k t", k=KD)
        qcT = SCR[:, 3072:4096].bitcast(BF16).rearrange("p (k t) -> p k t", k=KD)
        xnT = xs.rearrange("p (k t) -> p k t", k=KD)
        gate_w = SCR[:, 4096:4096 + KD * E_N].rearrange("p (k e) -> p k e", k=KD)
        oh_lane = mag.bitcast(BF16)[:, 0:T * TOPK * P].rearrange("p (n l) -> p n l", l=P)
        oh_tile = cs[:, 0:T * TOPK * NTP // 2].bitcast(BF16).rearrange("p (n l) -> p n l", l=NTP)
        ohv = cs[:, 384:384 + T * TOPK * NTP * TABS // 2].bitcast(BF16).rearrange("p (n a l) -> p n a l", a=TABS, l=NTP)
        xg = [SCR[:, i * D:(i + 1) * D] for i in range(2)]
        xgT = [SCR[:, 512 + i * D:512 + (i + 1) * D].rearrange("p (k s) -> p k s", k=KD) for i in range(2)]
        g_s = SCR[:, 1024:1024 + M_F]
        hm = SCR[:, 1920:1920 + M_F]
        hT = SCR[:, 2816:2816 + M_F].rearrange("p (j s) -> p j s", j=JF)
        ys = [SCR[:, 3712 + i * D:3712 + (i + 1) * D] for i in range(2)]
        assert 3712 + 2 * D <= SCR.shape[1]

        XN_d = dram("xn_rows", [B * S, D])
        KP_d = dram("key_parts", [3, D, B * S], BF16)
        QP_d = dram("query_parts", [3, D, B * S], BF16)
        V_d = dram("values", [B * S, D])
        ROW_d = dram("mask_and_one_rows", [2, B * S], BF16)
        ACC_d = dram("residual_rows", [B * S + P, D])

        s_xh = sem("x_second_half_landed")
        s_x, s_c, s_g, s_gw = sem("x_landed"), sem("ctx_landed"), sem("gates_landed"), sem("gate_w_landed")
        s_w = [sem(f"expert{e}_landed") for e in range(E_N)]
        s_wr = sem("experts_ready")
        s_const = sem("constants_made")
        s_poolc = sem("pool_steps")
        s_v = sem("vector_steps")
        s_tg = sem("tanh_done")
        s_var = sem("variance_done")
        s_std = sem("std_done")
        s_amaxc = sem("ctx_block_max_done")
        s_allc = sem("ctx_max_over_partitions")
        s_qc, s_qx = sem("ctx_quantised"), sem("x_quantised")
        s_tr = sem("q_transposed")
        s_trc = sem("q_transposes_copied")
        s_xa = sem("cross_products_done")
        s_xn2 = sem("xn2_done")
        s_x2T, s_x2Tc = sem("xn2_transposed"), sem("xn2_transposes_copied")
        s_rt = sem("logits_done")
        s_hits = sem("hits_done")
        s_rank = sem("ranks_done")
        s_dl, s_ed = sem("logit_gap_done"), sem("gap_exp_done")
        s_oh = sem("slot_onehots_done")
        s_tokp = sem("slot_tokens_done")
        s_tab = sem("tile_tables_done")
        s_coef = sem("coefficients_made")
        s_scc, s_magc = sem("ctx_scaled"), sem("ctx_magic_made")
        s_blk = sem("first_blocks_weighed")
        s_cros = sem("second_blocks_weighed")
        s_eg, s_gv = sem("gates_made"), sem("gate_parts_made")
        s_tok, s_eid = sem("slot_tokens_listed"), sem("tile_experts_listed")
        s_xnd = sem("xn_rows_stored")
        s_scidx = sem("residual_index_copied")
        s_rows = [sem(f"rows_landed{i}") for i in range(2)]
        s_idx = sem("index_copied")
        s_xTp, s_xTs = sem("xT_in_psum"), sem("xT_in_sbuf")
        s_h1, s_h3 = sem("h1_done"), sem("h3_done")
        s_gs = sem("silu_done")
        s_hm = sem("hidden_done")
        s_hTp, s_hTs = sem("hT_in_psum"), sem("hT_in_sbuf")
        s_y, s_ys = sem("y_done"), sem("y_in_sbuf")
        s_x1, s_acc0 = sem("x1_done"), sem("residual_rows_stored")
        s_sc = sem("tile_added")
        s_moe = sem("expert_tiles_done")
        s_x2 = [sem(f"x2_landed{h}") for h in range(3)]
        s_out = sem("out_stored")

        s_kvw, s_mask = sem("kv_weights_landed"), sem("mask_landed")
        s_kvT, s_kvTc = sem("kv_transposed"), sem("kv_transposes_copied")
        s_kv, s_kvc = sem("kv_products_done"), sem("kv_products_copied")
        s_kpart = sem("key_parts_made")
        s_maskrow = sem("mask_row_made")
        s_kvst = sem("kv_stored")
        s_prew = sem("layer1_weights_landed")
        s_ffw = sem("ffn1_weights_landed")
        s_kp = sem("keys_packed")
        s_vr = sem("values_landed")
        s_wop = sem("wo_widened")
        s_l1T, s_l1Tc = sem("layer1_weights_transposed"), sem("layer1_transposes_copied")
        s_x3n = sem("x3n_done")
        s_x3T, s_x3Tc = sem("x3n_transposed"), sem("x3n_transposes_copied")
        s_q, s_qh, s_qp = sem("q_done"), sem("q_high_done"), sem("q_parts_done")
        s_qst, s_qpk = ([sem(f"{x}{h}") for h in range(2)] for x in ("q_parts_stored", "q_packed"))
        s_left = sem("earlier_tile_added")
        s_last = sem("last_tile_added")
        s_ffb = sem("ffn1_B_landed")
        s_A, s_D0, s_r, s_rp, s_an = (sem(x) for x in ("pv_copied", "sums_gathered", "sums_inverted", "inverses_spread", "halves_normalised"))
        s_spread = sem("spread_made")
        s_og = sem("out_gated")
        s_gt, s_gtc = sem("gate_product_done"), sem("gate_done")
        s_prep, s_preph, s_prepc = (sem(f"map_weights_{x}") for x in ("transposed", "high", "low"))
        s_xlo, s_ulo, s_vs = sem("x4T_low_done"), sem("uT_low_done"), sem("routed_sum_done")
        s_biasr, s_uTw = sem("bias_parts_done"), sem("uT_whole_copied")
        s_S, s_mx = sem("scores_done"), sem("score_max_done")
        s_nm, s_nmp, s_nmc, s_nmd = sem("max_parts_done"), sem("max_transposed"), sem("max_copied"), sem("max_rows_landed")
        s_ST, s_pt = sem("scoresT_done"), sem("probs_done")
        s_PV = sem("pv_done")
        s_vw = sem("values_widened")
        chain, chain2, chain4 = (sem(x) for x in ("max_part_steps", "normalise_steps", "route_steps"))
        s_O, s_oe = sem("o_done"), sem("o_added")
        s_xf, s_fT, s_fTc = sem("x4n_done"), sem("x4n_transposed"), sem("x4n_transposes_copied")
        s_V, s_sq, s_ar, s_pk = sem("vecs_done"), sem("squares_done"), sem("squares_read"), sem("vecs_read")
        s_u, s_uT, s_uTc = sem("u_done"), sem("u_transposed"), sem("u_transposes_copied")
        s_alone = sem("waits_that_stand_alone")
        s_D, s_fin = sem("ffn1_done"), sem("tile_final")

        block = ctx.enter_context(nc.Block())

        @block.sync
        def _(sp):
            for h in range(2):
                sp.dma_start(X[:, h * 4:h * 4 + 4, :], a["x"].rearrange("b (t p) d -> p (b t) d", p=P)[:, h * 4:h * 4 + 4, :]).then_inc((s_x, s_xh)[h], 16)
            sp.dma_start(ctx_rows.rearrange("p (t d) -> p t d", d=D),
                         a["ctx_2048"].rearrange("b (t p) d -> p (b t) d", p=P)).then_inc(s_c, 16)
            sp.dma_start(gates[:, 0:2], a["g_xattn"].unsqueeze(0).to_broadcast([P, 2])).then_inc(s_g, 16)
            sp.dma_start(gates[:, 2:4], a["g_ffn"].unsqueeze(0).to_broadcast([P, 2])).then_inc(s_g, 16)
            sp.dma_start(gate_w, a["L0_ffn_gate_w"].rearrange("(k p) e -> p k e", p=P)).then_inc(s_gw, 16)

            for n, w in enumerate(("L1_xattn_wk", "L1_xattn_wv")):
                sp.dma_start(kv_raw[:, n, :, :], a[w].rearrange("(t p) d -> p t d", p=P)).then_inc(s_kvw, 16)
            sp.dma_start(mask_u8, a["mask_BxS2_bk0"].rearrange("b s -> (b s)").unsqueeze(0)).then_inc(s_mask, 16)
            sp.dma_start(nw, a["L1_xattn_norm_w"].rearrange("(k p) -> p k", p=P), allow_slow_non_contiguous=True).then_inc(s_mask, 16)
            sp.dma_start(bias_row[0:1, :], a["L1_ffn_bias"].unsqueeze(0)).then_inc(s_mask, 16)

            def load_expert(e, paced=False):
                h = KD * M_F
                for n, w in enumerate(("L0_ffn_w1", "L0_ffn_w3")):
                    sp.dma_start(wt(e)[:, n * h:(n + 1) * h].rearrange("p (k f) -> p k f", k=KD),
                                 a[w][e].rearrange("(k p) f -> p k f", p=P)).then_inc(s_w[e], 16)
                    if paced:
                        sp.wait_ge(s_w[e], 16 * (n + 1))
                sp.dma_start(wt(e)[:, 2 * h:WE].rearrange("p (j d) -> p j d", j=JF),
                             a["L0_ffn_w2"][e].rearrange("(j p) d -> p j d", p=P)).then_inc(s_w[e], 16)
                if paced:
                    sp.wait_ge(s_w[e], 48)

            for e in range(E_N - LATE):
                load_expert(e)
            sp.wait_ge(s_x1, T)
            sp.dma_start(ACC_d[0:B * S, :].rearrange("(t p) d -> p t d", p=P), X[:, :, :]).then_inc(s_acc0, 16)
            sp.dma_start(ACC_d[B * S:B * S + P, :], X[:, 0, :]).then_inc(s_acc0, 16)
            sp.wait_ge(s_xn2, 2)
            sp.dma_start(XN_d.rearrange("(t p) d -> p t d", p=P), xn.rearrange("p (t d) -> p t d", d=D)).then_inc(s_xnd, 16)
            for e in range(E_N - LATE):
                sp.wait_ge(s_w[e], 48)
                sp.sem_inc(s_wr, 1)
            sp.wait_ge(s_rows[0], 16)
            sp.wait_ge(s_rows[1], 16)
            sp.wait_ge(s_kpart, 3)
            sp.dma_start(KP_d.rearrange("j (c p) t -> p (j c) t", p=P),
                         k_parts.rearrange("p j (c t) -> p (j c) t", c=KD)).then_inc(s_kvst, 16)
            sp.wait_ge(s_kvc, 8)
            sp.dma_start(V_d.rearrange("(t p) d -> p t d", p=P), v32.rearrange("p (t d) -> p t d", d=D)).then_inc(s_kvst, 16)
            sp.wait_ge(s_maskrow, 1)
            sp.dma_start(ROW_d[0:1, :], mask_row).then_inc(s_kvst, 16)
            sp.dma_start(ROW_d[1:2, :], one_row).then_inc(s_kvst, 16)
            sp.wait_ge(s_tokp, 1)
            sp.wait_ge(s_eid, 1)
            sp.wait_ge(s_xnd, 16)
            sp.wait_ge(s_kvst, 64)
            for e in range(E_N - LATE, E_N):
                load_expert(e, True)
                sp.sem_inc(s_wr, 1)
            sp.wait_ge(s_moe, 1)
            for n, w in enumerate(("L1_xattn_wq", "L1_xattn_wg", "L1_xattn_wo")):
                sp.dma_start(l1_raw[:, n, :, :], a[w].rearrange("(t p) d -> p t d", p=P)).then_inc(s_prew, 16)
            sp.wait_ge(s_last, 1)
            for i, tiles in enumerate(CHUNKS):
                t0, t1 = tiles[0], tiles[-1] + 1
                sp.dma_start(X[:, t0:t1, :], ACC_d[t0 * P:t1 * P, :].rearrange("(t p) d -> p t d", p=P)).then_inc(s_x2[i], 16)
            for n, j in enumerate(K_PART):
                sp.dma_start(Kp[n * HD:(n + 1) * HD, :, :], KP_d[j].rearrange("(h d) t -> d h t", d=HD)).then_inc(s_kp, 16)
            sp.dma_start(Kp[ROWS_QK:ROWS_S, :, :], ROW_d[0:1, :].unsqueeze(1).to_broadcast([1, NH, B * S])).then_inc(s_kp, 16)
            sp.dma_start(Kp[ROWS_S:ROWS_ST, :, :], ROW_d[1:2, :].unsqueeze(1).to_broadcast([3, NH, B * S])).then_inc(s_kp, 16)
            sp.dma_start(Qp[ROWS_QK:ROWS_S, :, :], ROW_d[1:2, :].unsqueeze(1).to_broadcast([1, NH, B * S])).then_inc(s_kp, 16)
            sp.dma_start(v_rows.rearrange("p (t d) -> p t d", d=D), V_d.rearrange("(t p) d -> p t d", p=P)).then_inc(s_vr, 16)
            for h, (tiles, made) in enumerate(((FIRST, 2), (OTHERS, 6))):
                part = slice(tiles[0] * P, (tiles[-1] + 1) * P)
                sp.wait_ge(s_qp, made)
                for j in range(3):
                    sp.dma_start(QP_d[j].rearrange("(c p) t -> p c t", p=P)[:, :, part],
                                 q_parts[:, j, :].rearrange("p (c t) -> p c t", c=KD)[:, :, part]).then_inc(s_qst[h], 16)
                sp.wait_ge(s_qst[h], 48)
                for n, j in enumerate(Q_PART):
                    sp.dma_start(Qp[n * HD:(n + 1) * HD, :, part], QP_d[j].rearrange("(h d) t -> d h t", d=HD)[:, :, part]).then_inc(s_qpk[h], 16)
            def max_rows(b):
                sp.wait_ge(s_nmc, b + 1)
                for j in range(3):
                    sp.dma_start(Qp[ROWS_S + j:ROWS_S + j + 1, :, bass.ds(b * S, S)], mT[j * NH:(j + 1) * NH, :]).then_inc(s_nmd, 16)

            max_rows(0)
            sp.dma_start(a_raw, a["L1_ffn_A"].rearrange("a r d -> (a r) d").rearrange("(j p) d -> p j d", p=P)).then_inc(s_ffw, 16)
            sp.dma_start(w_raw, a["L1_ffn_W"].rearrange("(t p) d -> p t d", p=P)).then_inc(s_ffw, 16)
            for j in range(KD):
                sp.dma_start(b_raw[:, j, :].rearrange("p (a r) -> p a r", r=NR),
                             a["L1_ffn_B"][:, j * P:(j + 1) * P, :].rearrange("a p r -> p a r")).then_inc(s_ffb, 16)
            with sp.Fori(1, B) as b:
                max_rows(b)

            def store(t):
                sp.wait_ge(s_fin, t + 1)
                sp.dma_start(out.rearrange("b s d -> (b s) d")[bass.ds(t * P, P), :], X[:, bass.ds(t, 1), :].rearrange("p t d -> p (t d)")).then_inc(s_out, 16)

            with sp.Fori(0, T) as t:
                store(t)
            sp.wait_ge(s_out, 16 * T)

        @block.gpsimd
        def _(pool):
            steps = [0]

            def link(ins):
                steps[0] += 1
                ins.then_inc(s_poolc, 1)
                pool.wait_ge(s_poolc, steps[0])

            nc.gpsimd.memset(ident_bf[:, :], 0.0)
            nc.gpsimd.memset(ones_bf[:, :], 1.0)
            link(nc.gpsimd.memset(ident[:, :], 0.0))
            nc.gpsimd.affine_select(out=ident[:, :], in_=ident[:, :], compare_op=ALU.not_equal, fill=1.0,
                                    base=0, pattern=[[-1, P]], channel_multiplier=1)
            nc.gpsimd.affine_select(out=ident_bf[:, :], in_=ident_bf[:, :], compare_op=ALU.not_equal, fill=1.0,
                                    base=0, pattern=[[-1, P]], channel_multiplier=1)
            nc.gpsimd.affine_select(out=before_bf[:, :], in_=ones_bf[:, :], compare_op=ALU.is_ge, fill=0.0,
                                    base=-1, pattern=[[1, P]], channel_multiplier=-1)
            nc.gpsimd.iota(iota_lane[:, :], pattern=[[1, P]], base=0, channel_multiplier=0,
                           allow_small_or_imprecise_dtypes=True)
            nc.gpsimd.iota(tile_no, pattern=[[1, NTP]], base=0, channel_multiplier=0,
                           allow_small_or_imprecise_dtypes=True)
            nc.gpsimd.iota(choice_tile.rearrange("p (t k) -> p t k", k=TOPK), pattern=[[1, T], [0, TOPK]], base=0, channel_multiplier=0,
                           allow_small_or_imprecise_dtypes=True)
            nc.gpsimd.iota(cmp64.rearrange("p (e j) -> p e j", e=E_N), pattern=[[0, E_N], [P, T]], base=0, channel_multiplier=0,
                           allow_small_or_imprecise_dtypes=True)
            link(nc.gpsimd.memset(sum_cols[:, :], 0.0))
            diagonal = sum_cols[:, :].rearrange("p (c x) -> p c x", c=NC)[:, :, 0:HC]
            nc.gpsimd.affine_select(out=diagonal, in_=diagonal, compare_op=ALU.not_equal, fill=1.0,
                                    base=-HD, pattern=[[0, NC], [-32, HC]], channel_multiplier=1)
            nc.gpsimd.iota(dummy_row, pattern=[[0, 1]], base=B * S, channel_multiplier=1,
                           allow_small_or_imprecise_dtypes=True)
            nc.gpsimd.iota(pcol[:, :], pattern=[[0, 1]], base=0, channel_multiplier=1,
                           allow_small_or_imprecise_dtypes=True).then_inc(s_const, 1)
            pool.wait_ge(s_amaxc, 1)
            nc.gpsimd.partition_all_reduce(amax_ca, amax_c, P, RMAX).then_inc(s_allc, 1)

            pool.wait_ge(s_const, 1)
            nc.gpsimd.tensor_copy(values[:, :, 0], pcol[:, 0:1].to_broadcast([P, T * TOPK]))
            nc.gpsimd.tensor_copy(values[:, :, 1], choice_tile)
            nc.gpsimd.memset(values[:, :, 5], 1.0)
            nc.gpsimd.tensor_copy(lane_no_bf, iota_lane[:, :])
            nc.gpsimd.tensor_copy(tile_no_bf, tile_no)
            pool.wait_ge(s_scc, 1)
            nc.gpsimd.tensor_tensor(cs.rearrange("p (n l) -> p n l", l=P), ctx_rows.rearrange("p (n l) -> p n l", l=P),
                                    bc(qs_c, P), ALU.mult).then_inc(s_scc, 1)
            pool.wait_ge(s_magc, 1)
            link(nc.gpsimd.tensor_tensor(cs, cs, mag_c, ALU.add))
            nc.gpsimd.tensor_tensor(qc_bf, cs, mag_c, ALU.subtract).then_inc(s_qc, 1)
            for t in range(T):
                pool.wait_ge(s_cros, t + 1)
                nc.gpsimd.tensor_tensor(X[:, t, :], X[:, t, :], mag[:, t * D:(t + 1) * D], ALU.add).then_inc(s_x1, 1)

            def gate_parts():
                pool.wait_ge(s_eg, 1)
                link(nc.gpsimd.tensor_scalar(gate_rest.rearrange("p (t k) -> p t k", k=TOPK), wtk.rearrange("p (k t) -> p t k", k=TOPK),
                                             tg[:, 2:3], None, ALU.mult))
                for j in range(3):
                    last = nc.gpsimd.tensor_copy(values[:, :, 2 + j], gate_rest)
                    if j < 2:
                        link(last)
                        link(nc.gpsimd.tensor_tensor(gate_rest, gate_rest, values[:, :, 2 + j], ALU.subtract))
                last.then_inc(s_gv, 1)

            for c in range(KD):
                half = slice(c * B * S, (c + 1) * B * S)
                pool.wait_ge(s_kvc, 2 * c + 2)
                link(nc.gpsimd.tensor_copy(k_parts[:, 0, half], k32[:, half]))
                link(nc.gpsimd.tensor_tensor(k32[:, half], k32[:, half], k_parts[:, 0, half], ALU.subtract))
                if c == KD - 1:
                    gate_parts()
                link(nc.gpsimd.tensor_copy(k_parts[:, 1, half], k32[:, half]))
                nc.gpsimd.tensor_tensor(k_parts[:, 2, half], k32[:, half], k_parts[:, 1, half], ALU.subtract).then_inc(s_kpart, 1)
            nc.gpsimd.memset(ones_row[0:1, :], 1.0).then_inc(s_kpart, 1)

            pool.wait_ge(s_mask, 48)
            pool.wait_ge(s_kvTc, 2)
            nc.gpsimd.memset(one_row, 1.0)
            nc.gpsimd.tensor_scalar(mask_row, mask_u8, -MASKED, MASKED, ALU.mult, ALU.add).then_inc(s_maskrow, 1)

            pool.wait_ge(s_tok, 1)
            pool.wait_ge(s_xnd, 16)

            def fetch(i, u, n):
                if n is not None:
                    pool.wait_ge(s_xTp, n)
                nc.gpsimd.tensor_copy(idx_col[:, u:u + 1], tok_i[:, bass.ds(i, 1)]).then_inc(s_idx, 1)
                pool.wait_ge(s_idx, i + 1)
                pool.sem_inc(s_alone, 1)
                nc.gpsimd.indirect_dma_start(xg[u], None, XN_d[:, :], bass.IndirectOffsetOnAxis(ap=idx_col[:, u:u + 1], axis=0)).then_inc(s_rows[u], 16)

            def add(i, u, first=False):
                nc.gpsimd.tensor_copy(sc_col[:, u:u + 1], sc_i[:, bass.ds(i, 1)]).then_inc(s_scidx, 1)
                pool.wait_ge(s_scidx, i + 1)
                pool.wait_ge(s_ys, i + 2)
                if not first:
                    pool.wait_ge(s_sc, 16 * i)
                pool.sem_inc(s_left, 1)
                nc.gpsimd.indirect_dma_start(ACC_d[:, :], bass.IndirectOffsetOnAxis(ap=sc_col[:, u:u + 1], axis=0), ys[u], None,
                                             compute_op=ALU.add).then_inc(s_sc, 16)

            pool.wait_ge(s_acc0, 32)
            pool.wait_ge(s_eid, 1)
            last_tile = pool.value_load(last_i[0:1, 0:1], min_val=NT_MIN, max_val=NT - 1)
            fetch(0, 0, None)
            fetch(1, 1, None)
            fetch(2, 0, 1)
            pool.wait_ge(s_tab, 1)
            add(0, 0, True)
            fetch(3, 1, 2)
            add(1, 1)
            with pool.Fori(3, NT - 1, 2) as i:
                with pool.If(i < last_tile):
                    fetch(i + 1, 0, i)
                    add(i - 1, 0)
                    fetch(i + 2, 1, i + 1)
                    add(i, 1)
            add(last_tile, 0)
            pool.wait_ge(s_sc, 16 * last_tile + 16)
            pool.sem_inc(s_last, 1)
            nc.gpsimd.memset(inv, 0.0)
            link(nc.gpsimd.memset(spread, 0.0))
            heads = spread.rearrange("p c (h w) -> p c h w", w=32)
            nc.gpsimd.affine_select(out=heads, in_=heads, compare_op=ALU.not_equal, fill=1.0,
                                    base=0, pattern=[[-HC, NC], [-1, HC], [0, 32]], channel_multiplier=1).then_inc(s_spread, 1)
            link(nc.gpsimd.memset(v_wide, 1.0))
            link(nc.gpsimd.memset(wo_wide, 0.0))
            pool.wait_ge(s_prew, 48)
            nc.gpsimd.tensor_copy(wo_wide[:, :, :, 0:HD], l1_raw[:, 2, :, :].rearrange("p t (h d) -> p t h d", d=HD)).then_inc(s_wop, 1)

            def widen_values(b):
                nc.gpsimd.tensor_copy(v_wide[:, :, :, 0:HD],
                                      v_rows[:, bass.ds(b * TB * D, TB * D)].rearrange("p (m h d) -> p m h d", m=TB, d=HD)).then_inc(s_vw, 1)

            pool.wait_ge(s_vr, 16)
            widen_values(0)
            def add_out(b):
                pool.wait_ge(s_og, b + 1)
                xb = X[:, bass.ds(b * TB, TB), :].rearrange("p t d -> p (t d)")
                nc.gpsimd.tensor_tensor(xb, xb, o_tmp, ALU.add).then_inc(s_oe, 1)

            with pool.Fori(1, B) as b:
                pool.wait_ge(s_PV, b * 8)
                widen_values(b)
                add_out(b - 1)

            def x4T_low(t, u):
                pool.wait_ge(s_fTc, t + 1)
                nc.gpsimd.tensor_tensor(x4T_lo[u], x4T_whole[u], x4T[u].bitcast(F32), ALU.subtract).then_inc(s_xlo, 1)

            def routed(t, u):
                pool.wait_ge(s_vs, t + 1)
                if not isinstance(t, int) or t:
                    pool.wait_ge(s_uT, 2 * t)
                nc.gpsimd.tensor_tensor(u_s.rearrange("p (a r) -> p a r", r=NR), bc(routes[u], NR),
                                        v_sum[u].unsqueeze(1).to_broadcast([P, NA, NR]), ALU.mult).then_inc(s_u, 1)

            def uT_low(t):
                for h in range(2):
                    pool.wait_ge(s_uTw, 2 * t + h + 1)
                    half = slice(4 * h, 4 * h + 4)
                    nc.gpsimd.tensor_tensor(uT_lo[:, half, :], uT_whole[:, half, :], uT[:, half, :].bitcast(F32), ALU.subtract).then_inc(s_ulo, 1)

            def maps(t, u, ahead=3):
                routed(t, u)
                if isinstance(t, int) and t == 0:
                    add_out(B - 1)
                uT_low(t)
                if ahead >= 3:
                    x4T_low(t + 3, 1 - u)

            x4T_low(0, 0)
            x4T_low(1, 1)
            x4T_low(2, 0)
            maps(0, 0)
            maps(1, 1)
            with pool.Fori(2, T - 4, 2) as t:
                maps(t, 0)
                maps(t + 1, 1)
            maps(T - 4, 0)
            maps(T - 3, 1, 2)
            maps(T - 2, 0, 1)
            maps(T - 1, 1, 0)

        @block.scalar
        def _(act):
            act.wait_ge(s_g, 32)
            nc.scalar.activation(tg[:, :], gates[:, :], ACT.Tanh).then_inc(s_tg, 1)
            act.wait_ge(s_var, 1)
            nc.scalar.activation(rstd[:, :], mv[:, :, 1], ACT.Sqrt, bias=eps_ln[:, 0:1]).then_inc(s_std, 1)
            act.wait_ge(s_kvT, 1)
            for n in range(2):
                nc.scalar.activation(kv_wT[:, n, :, :], psum[n].rearrange("p (k c) -> p k c", k=KD), ACT.Copy).then_inc(s_kvTc, 1)
            act.wait_ge(s_kvT, 2)
            for n in range(4):
                nc.scalar.activation(ctxT[:, n // 2, (n % 2) * BANK:(n % 2 + 1) * BANK], psum[2 + n], ACT.Copy).then_inc(s_kvTc, 1)
            for n, bank in enumerate((0, 1, 6, 7)):
                act.wait_ge(s_kv, n + 1)
                nc.scalar.activation(k32[:, n * BANK:(n + 1) * BANK], psum[bank], ACT.Copy).then_inc(s_kvc, 1)
            act.wait_ge(s_tr, 1)
            for k in range(KD):
                nc.scalar.activation(qxT[:, k, :], psbf[4 + k][:, 0:T * P], ACT.Copy).then_inc(s_trc, 1)
            act.wait_ge(s_tr, 2)
            nc.scalar.activation(qcT[:, 0, :], psbf[2][:, 0:T * P], ACT.Copy).then_inc(s_trc, 1)

            def root(n, tiles):
                t = slice(tiles[0], tiles[-1] + 1)
                act.wait_ge(s_var, n)
                nc.scalar.activation(rstd[:, t], mv[:, t, 1], ACT.Sqrt, bias=eps_ln[:, 0:1]).then_inc(s_std, 1)

            act.wait_ge(s_qc, 1)
            act.wait_ge(s_coef, 1)
            for t in range(T):
                act.wait_ge(s_xa, t + 1)
                for n in range(TB):
                    last = nc.scalar.activation(cs[:, t * D + n * P:t * D + (n + 1) * P], psum[t][:, n * P:(n + 1) * P], ACT.Copy,
                                                scale=coef[:, t, 0, n:n + 1])
                last.then_inc(s_blk, 1)
            root(2, EARLY)
            def copy_values(n):
                act.wait_ge(s_kv, n + 5)
                nc.scalar.activation(v32[:, n * BANK:(n + 1) * BANK], psum[n], ACT.Copy).then_inc(s_kvc, 1)

            copy_values(0)
            copy_values(1)
            for n in range(4):
                if n == KD:
                    root(3, REST)
                act.wait_ge(s_x2T, n + 1)
                nc.scalar.activation(xnT[:, n % 2, (n // 2) * BANK:(n // 2 + 1) * BANK], psum[X2_BANK[n // 2] + n % 2], ACT.Copy).then_inc(s_x2Tc, 1)
            act.wait_ge(s_dl, 1)
            nc.scalar.activation(wtk[:, 0:T], wtk[:, 0:T], ACT.Exp).then_inc(s_ed, 1)
            copy_values(2)
            copy_values(3)
            act.wait_ge(s_eid, 1)

            def silu(i):
                act.wait_ge(s_h1, i + 1)
                act.wait_ge(s_hm, i)
                for h in range(2):
                    last = nc.scalar.activation(g_s[:, h * MH:(h + 1) * MH], psum[h][:, 0:MH], ACT.Silu)
                last.then_inc(s_gs, 1)

            def copy_xT(i, u):
                act.wait_ge(s_xTp, i + 1)
                nc.scalar.activation(xgT[u], psum[6][:, 0:D].rearrange("p (k s) -> p k s", k=KD), ACT.Copy).then_inc(s_xTs, 1)

            def weigh_y(i, u, first=False):
                act.wait_ge(s_y, i + 2)
                if not first:
                    act.wait_ge(s_left, i)
                nc.scalar.activation(ys[u], psum[7][:, 0:D], ACT.Copy, scale=slot_gate[:, bass.ds(i, 1)]).then_inc(s_ys, 1)

            act.sem_inc(s_ys, 1)
            last_tile = act.value_load(last_i[0:1, 0:1], min_val=NT_MIN, max_val=NT - 1)
            copy_xT(0, 0)
            act.wait_ge(s_h1, 1)
            for h in range(2):
                last = nc.scalar.activation(g_s[:, h * MH:(h + 1) * MH], psum[h][:, 0:MH], ACT.Silu)
            last.then_inc(s_gs, 1)
            copy_xT(1, 1)
            silu(1)
            copy_xT(2, 0)
            act.wait_ge(s_tab, 1)
            weigh_y(0, 0, True)
            silu(2)
            copy_xT(3, 1)
            weigh_y(1, 1, True)
            with act.Fori(3, NT - 1, 2) as i:
                with act.If(i < last_tile):
                    silu(i)
                    copy_xT(i + 1, 0)
                    weigh_y(i - 1, 0)
                    silu(i + 1)
                    copy_xT(i + 2, 1)
                    weigh_y(i, 1)
            weigh_y(last_tile, 0)
            nc.scalar.activation(root_spare, eps_ln[:, 0:1], ACT.Sqrt)

            act.wait_ge(s_l1T, 1)
            for n in range(2):
                nc.scalar.activation(qg_wT[:, n, :, :], psum[n].rearrange("p (k c) -> p k c", k=KD), ACT.Copy).then_inc(s_l1Tc, 1)
            def root_rms(n, tiles):
                t = slice(tiles[0], tiles[-1] + 1)
                act.wait_ge(s_var, n)
                nc.scalar.activation(rms[:, t], rms[:, t], ACT.Sqrt).then_inc(s_std, 1)

            root(4, FIRST)
            root_rms(5, FIRST)
            for i, tiles in enumerate(CHUNKS):
                at, n = tiles[0] * P, len(tiles) * P
                for k in range(KD):
                    act.wait_ge(s_x3T, 2 * i + k + 1)
                    nc.scalar.activation(x3T[:, k, at:at + n], psum[X3_BANK[i] + k][:, 0:n], ACT.Copy,
                                         scale=nw[:, k:k + 1]).then_inc(s_x3Tc, 1)
                if i == 0:
                    root(6, OTHERS)
                    root_rms(7, OTHERS)
                for c in range(KD):
                    act.wait_ge(s_q, 2 * i + c + 1)
                    nc.scalar.activation(q_parts[:, 0, c * B * S + at:c * B * S + at + n], psum[Q_BANK[i] + c][:, 0:n], ACT.Copy, scale=ATT_SCALE).then_inc(s_qh, 1)
            for n in range(4):
                act.wait_ge(s_gt, n + 1)
                nc.scalar.activation(gate_s[:, n * BANK:(n + 1) * BANK], psum[4 + n], ACT.Sigmoid).then_inc(s_gtc, 1)
            act.wait_ge(s_l1T, 2)
            for n in range(2):
                nc.scalar.activation(wo_wT[:, 2 * n:2 * n + 2, :], psum[2 + n].rearrange("p (c o) -> p c o", c=2), ACT.Copy).then_inc(s_l1Tc, 1)

            def copy_x4T(t, u, bank=4, at=0):
                act.wait_ge(s_fT, t + 1)
                if not isinstance(t, int) or t >= 2:
                    act.wait_ge(s_xlo, t - 1)
                src = psum[bank][:, at:at + D].rearrange("p (k s) -> p k s", k=KD)
                nc.scalar.activation(x4T_whole[u], src, ACT.Copy)
                nc.scalar.activation(x4T[u], src, ACT.Copy).then_inc(s_fTc, 1)

            def map_weights(n):
                act.wait_ge(s_prep, n + 1)
                nc.scalar.activation(prep_dst[n], psum[n % 2], ACT.Copy, scale=prep_scale[n]).then_inc(s_preph, 1)

            def exps(b, u):
                for hp in range(NH // 2):
                    g = b * 8 + hp
                    act.wait_ge(s_ST, g + 1)
                    if not isinstance(g, int) or g >= 2:
                        act.wait_ge(s_PV, g - 1)
                    v = 2 + 2 * (hp % 2)
                    nc.scalar.activation(probs[hp % 2].rearrange("p g m l -> p (g m l)"), PS[:, v * BANK:(v + 2) * BANK], ACT.Exp).then_inc(s_pt, 1)
                    if hp % 2 == 0 and hp:
                        copy_chunk(b, hp // 2 - 1, u)
                    if isinstance(b, int) and b == B - 1 and hp < len(prep_dst) - 2:
                        map_weights(hp)
                    if isinstance(b, int) and b == B - 1 and hp == 2:
                        root(8, EARLY)
                if isinstance(b, int) and b == B - 1:
                    for n in range(len(prep_dst) - 2, len(prep_dst)):
                        map_weights(n)
                    act.wait_ge(s_fT, 2)
                    copy_x4T(0, 0, 1, 0)
                    copy_x4T(1, 1, 1, D)
                copy_chunk(b, 3, u)

            def copy_chunk(b, c, u):
                act.wait_ge(s_PV, b * 8 + 2 * c + 2)
                if c == 0 and (not isinstance(b, int) or b >= 2):
                    act.wait_ge(s_O, b - 1)
                nc.scalar.activation(attn[u][:, c, :], psum[6][:, 0:S], ACT.Copy).then_inc(s_A, 1)

            exps(0, 0)
            with act.Fori(1, B - 2, 2) as b:
                exps(b, 1)
                exps(b + 1, 0)
            exps(B - 1, 1)

            def squares(t, u):
                act.wait_ge(s_V, t + 1)
                if not isinstance(t, int) or t:
                    act.wait_ge(s_ar, t)
                nc.scalar.activation(vecs2, PS[:, 2 * u * BANK:(2 * u + 2) * BANK], ACT.Square).then_inc(s_sq, 1)

            def copy_uT(t):
                for h in range(2):
                    act.wait_ge(s_uT, 2 * t + h + 1)
                    if h == 0 and (not isinstance(t, int) or t):
                        act.wait_ge(s_D, t)
                    src = psum[4 + h].rearrange("p (j s) -> p j s", s=P)
                    nc.scalar.activation(uT[:, 4 * h:4 * h + 4, :], src, ACT.Copy).then_inc(s_uTc, 1)
                    nc.scalar.activation(uT_whole[:, 4 * h:4 * h + 4, :], src, ACT.Copy).then_inc(s_uTw, 1)

            def maps(t, u, ahead=3):
                if isinstance(t, int) and t == 1:
                    root(9, REST)
                copy_uT(t)
                if ahead >= 2:
                    squares(t + 2, u)
                if ahead >= 3:
                    copy_x4T(t + 3, 1 - u)

            squares(0, 0)
            copy_x4T(2, 0)
            squares(1, 1)
            maps(0, 0)
            maps(1, 1)
            with act.Fori(2, T - 4, 2) as t:
                maps(t, 0)
                maps(t + 1, 1)
            maps(T - 4, 0)
            maps(T - 3, 1, 2)
            maps(T - 2, 0, 1)
            maps(T - 1, 1, 0)

        @block.vector
        def _(v):
            steps = [0]

            def link(ins):
                steps[0] += 1
                ins.then_inc(s_v, 1)
                v.wait_ge(s_v, steps[0])

            def variances(tiles=range(T)):
                for t in tiles:
                    last = nc.vector.bn_stats(stats[:, t, :], X[:, t, :])
                link(last)
                for t in tiles:
                    last = nc.vector.bn_aggr(mv[:, t, :], stats[:, t, :])
                last.then_inc(s_var, 1)

            def invert_std(n, tiles=range(T)):
                v.wait_ge(s_std, n)
                t = slice(tiles[0], tiles[-1] + 1)
                link(nc.vector.reciprocal(rstd[:, t], rstd[:, t]))

            def norm_stats(n, tiles=range(T)):
                variances(tiles)
                invert_std(n, tiles)

            def normalise(dst, tiles=range(T)):
                for t in tiles:
                    last = nc.vector.tensor_scalar(dst[:, t * D:(t + 1) * D], X[:, t, :], mv[:, t, 0:1], rstd[:, t:t + 1],
                                                   ALU.subtract, ALU.mult)
                return last

            def block_scales(amax, eps, qs, ds):
                link(nc.vector.tensor_scalar(amax, amax, eps, None, ALU.max))
                nc.vector.tensor_scalar(ds, amax, 1.0 / FP8_MAX, None, ALU.mult)
                link(nc.vector.reciprocal(qs, amax))
                link(nc.vector.tensor_scalar(qs, qs, FP8_MAX, None, ALU.mult))

            def magic(m, scaled):
                link(nc.vector.tensor_scalar(m.bitcast(I32), scaled.bitcast(I32), 0x7F800000, None, ALU.bitwise_and))
                return nc.vector.tensor_scalar(m, m, 2.0 ** -6, 1.5 * 2.0 ** 20, ALU.max, ALU.mult)

            nc.vector.memset(ones8, 1.0)
            link(nc.vector.memset(eps_ln[:, :], LN_EPS))

            v.wait_ge(s_x, 16)
            for t in EARLY:
                nc.vector.bn_stats(stats[:, t, :], X[:, t, :])
            v.wait_ge(s_xh, 16)
            for t in REST:
                last = nc.vector.bn_stats(stats[:, t, :], X[:, t, :])
            link(last)
            for t in range(T):
                last = nc.vector.bn_aggr(mv[:, t, :], stats[:, t, :])
            last.then_inc(s_var, 1)
            v.wait_ge(s_c, 16)
            nc.vector.tensor_reduce(amax_c, ctx_rows.rearrange("p (n l) -> p n l", l=P), AX_X, ALU.max,
                                    apply_absolute_value=True).then_inc(s_amaxc, 1)
            invert_std(1)
            link(normalise(xn))
            v.wait_ge(s_allc, 1)
            block_scales(amax_ca, W_EPS, qs_c, ds_c)
            v.sem_inc(s_scc, 1)
            link(nc.vector.tensor_reduce(amax_x, xn.rearrange("p (n l) -> p n l", l=P), AX_X, ALU.max,
                                         apply_absolute_value=True))
            block_scales(amax_x, ACT_EPS, qs_x, ds_x)
            link(nc.vector.tensor_tensor(xs.rearrange("p (n l) -> p n l", l=P), xn.rearrange("p (n l) -> p n l", l=P),
                                         bc(qs_x, P), ALU.mult))
            v.wait_ge(s_scc, 2)
            magic(mag_c, cs).then_inc(s_magc, 1)
            link(magic(mag, xs))
            link(nc.vector.tensor_tensor(xs, xs, mag, ALU.add))
            nc.vector.tensor_tensor(qx_bf, xs, mag, ALU.subtract).then_inc(s_qx, 1)
            v.wait_ge(s_tg, 1)
            link(nc.vector.tensor_scalar(ds_x, ds_x, tg[:, 0:1], None, ALU.mult))
            dsc = ds_c.rearrange("p (b n k) -> p b k n", b=B, n=TB)
            for t in range(T):
                last = nc.vector.tensor_tensor(coef[:, t, :, :], bc(ds_x[:, t * KD:(t + 1) * KD], TB), dsc[:, t // TB, :, :], ALU.mult)
            last.then_inc(s_coef, 1)
            v.wait_ge(s_tr, 2)
            nc.vector.tensor_copy(qcT[:, 1, :], psbf[3][:, 0:T * P]).then_inc(s_trc, 1)
            v.wait_ge(s_coef, 1)

            def variance_steps(t):
                v.wait_ge(s_x1, t + 1)
                return nc.vector.bn_stats(stats[:, t, :], X[:, t, :])

            def aggregate(tiles):
                for t in tiles:
                    last = nc.vector.bn_aggr(mv[:, t, :], stats[:, t, :])
                last.then_inc(s_var, 1)

            for t in range(T):
                v.wait_ge(s_blk, t + 1)
                for n in range(TB):
                    part = slice(t * D + n * P, t * D + (n + 1) * P)
                    last = nc.vector.scalar_tensor_tensor(mag[:, part], psum[t][:, D + n * P:D + (n + 1) * P],
                                                          coef[:, t, 1, n:n + 1], cs[:, part], ALU.mult, ALU.add)
                last.then_inc(s_cros, 1)
                if 2 <= t < T // 2 + 2:
                    last = variance_steps(t - 2)
                if t == T // 2 + 1:
                    link(last)
                    aggregate(EARLY)

            invert_std(2, EARLY)
            normalise(xn, EARLY).then_inc(s_xn2, 1)
            for t in REST:
                last = variance_steps(t)
            link(last)
            aggregate(REST)
            invert_std(3, REST)
            normalise(xn, REST).then_inc(s_xn2, 1)
            v.wait_ge(s_rt, 1)
            link(nc.vector.tensor_copy(logits_v, psum[4][:, 0:T * E_N]))
            lg = logits_v.rearrange("p (t e) -> p t e", e=E_N)
            t8 = top8.rearrange("p (t e) -> p t e", e=8)
            t8i = top8i.rearrange("p (t e) -> p t e", e=8)
            t8f = top8f.rearrange("p (t e) -> p t e", e=8)
            for t in range(T):
                last = nc.vector.max(t8[:, t, :], lg[:, t, :])
            link(last)
            for t in range(T):
                last = nc.vector.max_index(t8i[:, t, :], t8[:, t, :], lg[:, t, :])
            link(last)
            nc.vector.tensor_tensor(wtk[:, 0:T], t8[:, :, 1], t8[:, :, 0], ALU.subtract).then_inc(s_dl, 1)
            link(nc.vector.tensor_copy(top8f, top8i))
            oh = onehot.rearrange("p (t k e) -> p t k e", t=T, k=TOPK)
            for k in range(TOPK):
                last = nc.vector.tensor_tensor(oh[:, :, k, :], iota_lane[:, 0:E_N].unsqueeze(1).to_broadcast([P, T, E_N]),
                                               bc(t8f[:, :, k], E_N), ALU.is_equal)
            link(last)
            nc.vector.tensor_tensor(hits_bf.rearrange("p (t e) -> p t e", e=E_N), oh[:, :, 0, :], oh[:, :, 1, :], ALU.add).then_inc(s_hits, 1)
            v.wait_ge(s_ed, 1)
            link(nc.vector.tensor_scalar(wtk[:, T:2 * T], wtk[:, 0:T], 1.0, None, ALU.add))
            link(nc.vector.reciprocal(top8f[:, 0:T], wtk[:, T:2 * T]))
            link(nc.vector.tensor_tensor(wtk[:, T:2 * T], wtk[:, 0:T], top8f[:, 0:T], ALU.mult))
            nc.vector.tensor_copy(wtk[:, 0:T], top8f[:, 0:T]).then_inc(s_eg, 1)
            v.wait_ge(s_rank, 1)
            c64 = cmp64.rearrange("p (e j) -> p e j", e=E_N)
            link(nc.vector.tensor_copy(tiles_c, psum[5][:, 64:64 + E_N]))
            link(nc.vector.tensor_tensor(c64, bc(tiles_c, T), c64, ALU.is_gt))
            link(nc.vector.tensor_reduce(tiles_e, c64, AX_X, ALU.add))
            link(nc.vector.tensor_tensor_scan(tiles_c, ones8, tiles_e, 0.0, ALU.mult, ALU.add))
            link(nc.vector.tensor_tensor(base_e, tiles_c, tiles_e, ALU.subtract))
            link(nc.vector.tensor_scalar(base_e, base_e, float(P), None, ALU.mult))
            se = slot_e.rearrange("p (t e) -> p t e", e=E_N)
            link(nc.vector.tensor_tensor(se, psum[5][:, 0:T * E_N].rearrange("p (t e) -> p t e", e=E_N),
                                         base_e.unsqueeze(1).to_broadcast([P, T, E_N]), ALU.add))
            pr = prod.rearrange("p (t k e) -> p t k e", t=T, k=TOPK)
            for k in range(TOPK):
                last = nc.vector.tensor_tensor(pr[:, :, k, :], oh[:, :, k, :], se, ALU.mult)
            link(last)
            link(nc.vector.tensor_reduce(slot_f, prod.rearrange("p (n e) -> p n e", e=E_N), AX_X, ALU.add))
            link(nc.vector.tensor_copy(slot_i, slot_f))
            nc.vector.tensor_scalar(tile_i, slot_i, 7, None, ALU.logical_shift_right)
            link(nc.vector.tensor_scalar(lane_i, slot_i, P - 1, None, ALU.bitwise_and))
            nc.vector.tensor_copy(tile_bf, tile_i)
            link(nc.vector.tensor_copy(lane_bf, lane_i))
            N2 = T * TOPK
            link(nc.vector.tensor_tensor(oh_tile, tile_no_bf.unsqueeze(1).to_broadcast([P, N2, NTP]), bc(tile_bf, NTP), ALU.is_equal))
            nc.vector.tensor_tensor(oh_lane, lane_no_bf.unsqueeze(1).to_broadcast([P, N2, P]), bc(lane_bf, P), ALU.is_equal)
            v.wait_ge(s_gv, 1)
            for entry in range(TABS):
                last = nc.vector.tensor_tensor(ohv[:, :, entry, :], oh_tile, bc(values[:, :, entry], NTP), ALU.mult)
            last.then_inc(s_oh, 1)
            ev = cs[:, 0:NTP * E_N].rearrange("p (i e) -> p i e", e=E_N)
            v.wait_ge(s_oh, 1)
            link(nc.vector.tensor_tensor(ev, bc(tile_no, E_N), tiles_c.unsqueeze(1).to_broadcast([P, NTP, E_N]), ALU.is_ge))
            link(nc.vector.tensor_reduce(eid_f, ev, AX_X, ALU.add))
            link(nc.vector.tensor_scalar(eid_f, eid_f, float(E_N - 1), None, ALU.min))
            link(nc.vector.tensor_copy(eid_i, eid_f))
            link(nc.vector.tensor_copy(count_i, tiles_c[:, E_N - 1:E_N]))
            nc.vector.tensor_scalar(last_i, count_i, 1, 1, ALU.logical_shift_right, ALU.logical_shift_left).then_inc(s_eid, 1)
            v.wait_ge(s_tokp, 1)
            tab = psum[6][:, 0:TABS * NTP].rearrange("p (a i) -> p a i", a=TABS)
            link(nc.vector.tensor_copy(tok_f, tab[:, 0, :]))
            link(nc.vector.scalar_tensor_tensor(tok_f, tab[:, 1, :], float(P), tok_f, ALU.mult, ALU.add))
            nc.vector.tensor_copy(tok_i, tok_f).then_inc(s_tok, 1)
            link(nc.vector.tensor_scalar(filled, tab[:, 5, :], dummy_row, None, ALU.mult))
            link(nc.vector.tensor_scalar(sc_f, tok_f, dummy_row, None, ALU.add))
            link(nc.vector.tensor_tensor(sc_f, sc_f, filled, ALU.subtract))
            link(nc.vector.tensor_copy(sc_i, sc_f))
            link(nc.vector.tensor_copy(slot_gate, tab[:, 2, :]))
            link(nc.vector.tensor_tensor(slot_gate, slot_gate, tab[:, 3, :], ALU.add))
            nc.vector.tensor_tensor(slot_gate, slot_gate, tab[:, 4, :], ALU.add).then_inc(s_tab, 1)
            v.wait_ge(s_eid, 1)

            def product(i):
                v.wait_ge(s_gs, i + 1)
                v.wait_ge(s_h3, i + 1)
                for h in range(2):
                    last = nc.vector.tensor_tensor(hm[:, h * MH:(h + 1) * MH], g_s[:, h * MH:(h + 1) * MH], psum[2 + h][:, 0:MH], ALU.mult)
                last.then_inc(s_hm, 1)

            def copy_hT(i):
                v.wait_ge(s_hTp, i + 1)
                nc.vector.tensor_copy(hT[:, 0:4, :], psum[4][:, :].rearrange("p (j s) -> p j s", s=P))
                nc.vector.tensor_copy(hT[:, 4:JF, :], psum[5][:, 0:(JF - 4) * P].rearrange("p (j s) -> p j s", s=P)).then_inc(s_hTs, 1)

            def copy_hT_later(i):
                v.wait_ge(s_y, i + 1)
                copy_hT(i)

            last_tile = v.value_load(last_i[0:1, 0:1], min_val=NT_MIN, max_val=NT - 1)
            product(0)
            copy_hT(0)
            product(1)
            copy_hT_later(1)
            product(2)
            with v.Fori(3, NT - 1, 2) as i:
                with v.If(i < last_tile):
                    copy_hT_later(i - 1)
                    product(i)
                    copy_hT_later(i)
                    product(i + 1)
            copy_hT_later(last_tile)

            def mean_square(n, tiles):
                t = slice(tiles[0], tiles[-1] + 1)
                invert_std(n, tiles)
                link(nc.vector.tensor_tensor(rms[:, t], rstd[:, t], rstd[:, t], ALU.mult))
                link(nc.vector.tensor_tensor(rms[:, t], rms[:, t], mv[:, t, 1], ALU.mult))
                nc.vector.tensor_scalar(rms[:, t], rms[:, t], RMS_EPS, None, ALU.add).then_inc(s_var, 1)

            def both_norms(n, tiles):
                t = slice(tiles[0], tiles[-1] + 1)
                v.wait_ge(s_std, n)
                link(nc.vector.reciprocal(rms[:, t], rms[:, t]))
                link(nc.vector.tensor_tensor(rstd[:, t], rstd[:, t], rms[:, t], ALU.mult))

            v.wait_ge(s_x2[0], 16)
            variances(FIRST)
            mean_square(4, FIRST)
            both_norms(5, FIRST)
            normalise(x3n, FIRST).then_inc(s_x3n, 1)
            for i in (1, 2):
                v.wait_ge(s_x2[i], 16)
            variances(OTHERS)
            mean_square(6, OTHERS)
            both_norms(7, OTHERS)
            for tiles in CHUNKS[1:]:
                normalise(x3n, tiles).then_inc(s_x3n, 1)
            for i, tiles in enumerate(CHUNKS):
                at, n = tiles[0] * P, len(tiles) * P
                for c in range(KD):
                    part, rest = slice(c * B * S + at, c * B * S + at + n), q_rest[c][:, 0:n]
                    v.wait_ge(s_qh, 2 * i + c + 1)
                    link(nc.vector.scalar_tensor_tensor(rest, psum[Q_BANK[i] + c][:, 0:n], ATT_SCALE, q_parts[:, 0, part], ALU.mult, ALU.subtract))
                    link(nc.vector.tensor_copy(q_parts[:, 1, part], rest))
                    nc.vector.tensor_tensor(q_parts[:, 2, part], rest, q_parts[:, 1, part], ALU.subtract).then_inc(s_qp, 1)

            nc.vector.tensor_copy(ones_part[0:1, :], ones_row[0:1, :])
            link(nc.vector.tensor_copy(bias_parts[0:1, 0:D], bias_row[0:1, :]))
            nc.vector.tensor_tensor(bias_parts[0:1, D:2 * D], bias_row[0:1, :], bias_parts[0:1, 0:D].bitcast(F32), ALU.subtract).then_inc(s_biasr, 1)

            def max_unit(b, n):
                v.wait_ge(s_S, b * 16 + n + 1)
                lt, hp = n % TB, n // TB
                nc.vector.tensor_reduce(mx[:, lt, 2 * hp:2 * hp + 2], psum[n % 2].rearrange("p (g m) -> p g m", g=2), AX_X, ALU.max).then_inc(s_mx, 1)

            def max_parts(b):
                c = b * 4
                v.wait_ge(s_mx, b * 16 + 16)
                nc.vector.tensor_scalar(mneg, mx, -1.0, NO_KEY, ALU.mult, ALU.min).then_inc(chain, 1)
                v.wait_ge(chain, c + 1)
                nc.vector.tensor_copy(mparts[:, :, 0, :], mneg).then_inc(chain, 1)
                v.wait_ge(chain, c + 2)
                nc.vector.tensor_tensor(mneg, mneg, mparts[:, :, 0, :], ALU.subtract).then_inc(chain, 1)
                v.wait_ge(chain, c + 3)
                nc.vector.tensor_copy(mparts[:, :, 1, :], mneg).then_inc(chain, 1)
                v.wait_ge(chain, c + 4)
                nc.vector.tensor_tensor(mparts[:, :, 2, :], mneg, mparts[:, :, 1, :], ALU.subtract).then_inc(s_nm, 1)

            def max_copy(b):
                v.wait_ge(s_nmp, b + 1)
                if not isinstance(b, int) or b:
                    v.wait_ge(s_nmd, 48 * b)
                nc.vector.tensor_copy(mT[0:3 * NH, :], psbf[0][0:3 * NH, 0:S]).then_inc(s_nmc, 1)

            def invert_sums(b):
                v.wait_ge(s_D0, b + 1)
                nc.vector.tensor_scalar(inv_raw[0:NH, :], psum[7][0:NH, 0:S], 1.0 / -MASKED, None, ALU.max).then_inc(chain2, 1)
                v.wait_ge(chain2, b + 1)
                nc.vector.reciprocal(inv[0:NH, :], inv_raw[0:NH, :]).then_inc(s_r, 1)

            def apply_inverses(b, g, u):
                v.wait_ge(s_rp, 2 * b + g + 1)
                half = attn[u][:, 2 * g:2 * g + 2, :].rearrange("p c l -> p (c l)")
                nc.vector.tensor_tensor(half, half, psum[7], ALU.mult).then_inc(s_an, 1)

            def gate_out(b):
                v.wait_ge(s_O, b + 1)
                if not isinstance(b, int) or b:
                    v.wait_ge(s_oe, b)
                nc.vector.scalar_tensor_tensor(o_tmp, psum[7], tg[:, 1:2], gate_s[:, bass.ds(b * TB * D, TB * D)], ALU.mult, ALU.mult).then_inc(s_og, 1)

            def map_weights(n):
                if n == len(prep_dst) - JA // 2:
                    v.wait_ge(s_vw, B)
                v.wait_ge(s_preph, n + 1)
                nc.vector.scalar_tensor_tensor(prep_lo[n], psum[n % 2], prep_scale[n], prep_dst[n].bitcast(F32), ALU.mult, ALU.subtract).then_inc(s_prepc, 1)

            def norm_tile(t, u):
                if not isinstance(t, int) or t >= 2:
                    v.wait_ge(s_fT, t - 1)
                nc.vector.tensor_scalar(x4n[u], X[:, bass.ds(t, 1), :].rearrange("p t d -> p (t d)"), mean_of(t), rstd[:, bass.ds(t, 1)],
                                        ALU.subtract, ALU.mult).then_inc(s_xf, 1)

            def mean_of(t):
                return mv[:, bass.ds(t, 1), 0:1].rearrange("p t o -> p (t o)")

            def attention(b, u, ahead=True):
                before = not isinstance(b, int) or b
                for hp in range(8):
                    if before and hp in (2, 3):
                        apply_inverses(b - 1, hp - 2, 1 - u)
                    for n in UNITS[hp][0] if ahead else []:
                        max_unit(b + 1, n)
                    if before and hp == 0:
                        invert_sums(b - 1)
                    for n in UNITS[hp][1] if ahead else []:
                        max_unit(b + 1, n)
                    if ahead and hp == LAST_UNITS:
                        max_parts(b + 1)
                    if ahead and hp == LAST_UNITS + 1:
                        max_copy(b + 1)
                    if not ahead and hp < len(prep_dst) - 2:
                        map_weights(hp)
                    if before and hp == 5:
                        gate_out(b - 1)
                    if not ahead and hp == 1:
                        v.wait_ge(s_oe, B // 2)
                        variances(EARLY)
                    if not ahead and hp == 4:
                        invert_std(8, EARLY)
                        norm_tile(0, 0)
                        norm_tile(1, 1)

            for n in range(16):
                max_unit(0, n)
            max_parts(0)
            max_copy(0)
            v.wait_ge(s_spread, 1)
            attention(0, 0)
            with v.Fori(1, B - 2, 2) as b:
                attention(b, 1)
                attention(b + 1, 0)
            attention(B - 1, 1, False)
            for n in range(len(prep_dst) - 2, len(prep_dst)):
                map_weights(n)
            invert_sums(B - 1)
            apply_inverses(B - 1, 0, 1)
            apply_inverses(B - 1, 1, 1)

            FS = 5

            def route(t, u):
                k = [0]

                def step(ins):
                    k[0] += 1
                    ins.then_inc(chain4, 1)
                    v.wait_ge(chain4, t * FS + k[0])
                    v.sem_inc(s_alone, 1)

                v.wait_ge(s_sq, t + 1)
                nc.vector.tensor_reduce(norm2, vecs2.rearrange("p (a r) -> p a r", r=NR), AX_X, ALU.add).then_inc(s_ar, 1)
                v.wait_ge(s_ar, t + 1)
                v.sem_inc(s_alone, 1)
                step(nc.vector.max(f_top, norm2))
                step(nc.vector.max_index(f_topi, f_top, norm2))
                step(nc.vector.tensor_copy(f_topf, f_topi))
                top = is_top.rearrange("p (a j) -> p a j", j=RTOP)
                step(nc.vector.tensor_tensor(top, bc(iota_lane[:, 0:NA], RTOP), f_topf[:, 0:RTOP].unsqueeze(1).to_broadcast([P, NA, RTOP]), ALU.is_equal))
                if not isinstance(t, int) or t >= 2:
                    v.wait_ge(s_u, t - 1)
                step(nc.vector.tensor_reduce(routes[u], top, AX_X, ALU.add))
                vec = PS[:, 2 * u * BANK:(2 * u + 2) * BANK]
                nc.vector.tensor_tensor(picked.rearrange("p (a r) -> p a r", r=NR), vec.rearrange("p (a r) -> p a r", r=NR),
                                        bc(routes[u], NR), ALU.mult).then_inc(s_pk, 1)
                v.wait_ge(s_pk, t + 1)
                nc.vector.tensor_reduce(v_sum[u], picked.rearrange("p (a r) -> p r a", r=NR), AX_X, ALU.add).then_inc(s_vs, 1)
                v.wait_ge(s_vs, t + 1)
                v.sem_inc(s_alone, 1)
                assert k[0] == FS

            def final(t, u):
                v.wait_ge(s_D, t + 1)
                xt = X[:, bass.ds(t, 1), :].rearrange("p t d -> p (t d)")
                nc.vector.scalar_tensor_tensor(xt, psum[6 + u][:, 0:D], tg[:, 3:4], xt, ALU.mult, ALU.add).then_inc(s_fin, 1)

            def maps(t, u, ahead=3):
                route(t, u)
                final(t - 1, 1 - u)
                if isinstance(t, int) and t == 1:
                    v.wait_ge(s_oe, B)
                    norm_stats(9, REST)
                if ahead >= 3:
                    norm_tile(t + 3, 1 - u)

            norm_tile(2, 0)
            route(0, 0)
            gate_out(B - 1)
            norm_tile(3, 1)
            maps(1, 1)
            with v.Fori(2, T - 4, 2) as t:
                maps(t, 0)
                maps(t + 1, 1)
            maps(T - 4, 0)
            maps(T - 3, 1, 2)
            maps(T - 2, 0, 1)
            maps(T - 1, 1, 0)
            final(T - 1, 1)

        @block.tensor
        def _(pe):
            pe.wait_ge(s_const, 1)
            pe.wait_ge(s_kvw, 32)
            for n in range(2):
                for k in range(KD):
                    for c in range(KD):
                        last = nc.tensor.transpose(psum[n][:, k * D + c * P:k * D + (c + 1) * P], kv_raw[:, n, c, k * P:(k + 1) * P], ident[:, :])
            last.then_inc(s_kvT, 1)
            pe.wait_ge(s_c, 16)
            for n in range(4):
                for t in range(4):
                    tt = (n % 2) * 4 + t
                    last = nc.tensor.transpose(psum[2 + n][:, t * P:(t + 1) * P], ctx_rows[:, tt * D + (n // 2) * P:tt * D + (n // 2 + 1) * P], ident[:, :])
            last.then_inc(s_kvT, 1)
            pe.wait_ge(s_kvTc, 6)
            for n, bank in enumerate((0, 1, 6, 7)):
                c, h = n // 2, n % 2
                for k in range(KD):
                    last = nc.tensor.matmul(psum[bank], kv_wT[:, 0, k, c * P:(c + 1) * P], ctxT[:, k, h * BANK:(h + 1) * BANK],
                                            start=(k == 0), stop=(k == KD - 1))
                last.then_inc(s_kv, 1)
            for g, (src, ready) in enumerate(((qx_bf, s_qx), (qc_bf, s_qc))):
                pe.wait_ge(ready, 1)
                for k in range(KD):
                    for t in range(T):
                        last = nc.tensor.transpose(psbf[(4, 2)[g] + k][:, t * P:(t + 1) * P], src[:, t * D + k * P:t * D + (k + 1) * P], ident_bf[:, :])
                last.then_inc(s_tr, 1)
            pe.wait_ge(s_kvc, 4)
            pe.wait_ge(s_trc, 2 * KD)
            for t in range(T):
                b = t // TB
                for k in range(KD):
                    last = nc.tensor.matmul(psum[t][:, k * D:(k + 1) * D], qxT[:, k, t * P:(t + 1) * P],
                                            qcT[:, k, b * S:(b + 1) * S], start=True, stop=True)
                last.then_inc(s_xa, 1)

            def value_products(n, bank):
                for t in (2 * n, 2 * n + 1):
                    for k in range(KD):
                        last = nc.tensor.matmul(psum[bank][:, (t % 2) * D:(t % 2 + 1) * D], ctxT[:, k, t * P:(t + 1) * P], kv_wT[:, 1, k, :],
                                                start=(k == 0), stop=(k == KD - 1))
                last.then_inc(s_kv, 1)

            for n in range(2):
                pe.wait_ge(s_cros, n + 1)
                value_products(n, n)
            pe.wait_ge(s_gw, 16)
            for h in range(2):
                pe.wait_ge(s_xn2, h + 1)
                for k in range(KD):
                    for t in range(4):
                        tt = 4 * h + t
                        last = nc.tensor.transpose(psum[X2_BANK[h] + k][:, t * P:(t + 1) * P], xn[:, tt * D + k * P:tt * D + (k + 1) * P], ident[:, :])
                    last.then_inc(s_x2T, 1)
            for h in range(2):
                pe.wait_ge(s_x2Tc, 2 * h + 2)
                for t in range(4 * h, 4 * h + 4):
                    for k in range(KD):
                        last = nc.tensor.matmul(psum[4][:, t * E_N:(t + 1) * E_N], xnT[:, k, t * P:(t + 1) * P], gate_w[:, k, :],
                                                start=(k == 0), stop=(k == KD - 1))
            last.then_inc(s_rt, 1)
            pe.wait_ge(s_hits, 1)
            hb = hits_bf.rearrange("p (t e) -> p t e", e=E_N)
            rank = psum[5][:, 0:T * E_N].rearrange("p (t e) -> p t e", e=E_N)
            nc.tensor.matmul(rank, before_bf[:, :], hb, start=True, stop=False, skip_group_check=True)
            for t in range(T - 1):
                nc.tensor.matmul(rank[:, t + 1:T, :], ones_bf[:, :], hb[:, t:t + 1, :].to_broadcast([P, T - 1 - t, E_N]),
                                 start=False, stop=(t == T - 2), skip_group_check=True)
            for t in range(T):
                last = nc.tensor.matmul(psum[5][:, 64:64 + E_N], ones_bf[:, :], hb[:, t, :], start=False, stop=(t == T - 1), skip_group_check=True)
            last.then_inc(s_rank, 1)
            for n in range(2, 4):
                value_products(n, n)
            pe.wait_ge(s_oh, 1)
            for n in range(T * TOPK):
                last = nc.tensor.matmul(psum[6][:, 0:TABS * NTP], oh_lane[:, n, :], ohv[:, n, :, :].rearrange("p a b -> p (a b)"),
                                        start=(n == 0), stop=(n == T * TOPK - 1))
            last.then_inc(s_tokp, 1)

            pe.wait_ge(s_eid, 1)
            pe.wait_ge(s_kvc, 8)
            pe.wait_ge(s_tab, 1)

            def expert(i):
                return pe.value_load(eid_i[0:1, bass.ds(i, 1)], min_val=0, max_val=E_N - 1)

            def transpose_x(i, u, landed):
                pe.wait_ge(s_rows[u], 16 * landed)
                for k in range(KD):
                    last = nc.tensor.transpose(psum[6][:, k * P:(k + 1) * P], xg[u][:, k * P:(k + 1) * P], ident[:, :])
                last.then_inc(s_xTp, 1)

            def up(i, u, e, n):
                for h in range(2):
                    for k in range(KD):
                        last = nc.tensor.matmul(psum[2 * n + h][:, 0:MH], xgT[u][:, k, :],
                                                W[:, bass.ds(e * WE + (n * KD + k) * M_F + h * MH, MH)],
                                                start=(k == 0), stop=(k == KD - 1))
                last.then_inc((s_h1, s_h3)[n], 1)

            def transpose_h(i):
                for j in range(JF):
                    last = nc.tensor.transpose(psum[4 + j // 4][:, (j % 4) * P:(j % 4 + 1) * P], hm[:, j * P:(j + 1) * P], ident[:, :])
                last.then_inc(s_hTp, 1)

            def down(i, e):
                pe.wait_ge(s_hTs, i + 1)
                pe.wait_ge(s_ys, i + 1)
                for j in range(JF):
                    last = nc.tensor.matmul(psum[7][:, 0:D], hT[:, j, :], W[:, bass.ds(e * WE + 2 * KD * M_F + j * D, D)],
                                            start=(j == 0), stop=(j == JF - 1))
                last.then_inc(s_y, 1)

            def tile(i, u, landed_next):
                e = expert(i)
                pe.wait_ge(s_xTs, i + 1)
                pe.wait_ge(s_wr, e + 1)
                pe.wait_ge(s_gs, i)
                up(i, u, e, 0)
                pe.wait_ge(s_hm, i)
                transpose_h(i - 1)
                up(i, u, e, 1)
                transpose_x(i + 1, 1 - u, landed_next)
                down(i - 1, expert(i - 1))

            last_tile = pe.value_load(last_i[0:1, 0:1], min_val=NT_MIN, max_val=NT - 1)
            pe.sem_inc(s_y, 1)
            transpose_x(0, 0, 1)
            e = expert(0)
            pe.wait_ge(s_xTs, 1)
            pe.wait_ge(s_wr, e + 1)
            up(0, 0, e, 0)
            up(0, 0, e, 1)
            transpose_x(1, 1, 1)
            tile(1, 1, 2)
            tile(2, 0, 2)
            with pe.Fori(3, NT - 1, 2) as i:
                with pe.If(i < last_tile):
                    half = pe.snap(i // 2)
                    tile(i, 1, half + 2)
                    tile(i + 1, 0, half + 2)
            pe.wait_ge(s_hm, last_tile + 1)
            transpose_h(last_tile)
            down(last_tile, expert(last_tile))
            pe.wait_ge(s_ys, last_tile + 2)
            pe.sem_inc(s_moe, 1)

            pe.wait_ge(s_prew, 48)
            for n in range(2):
                for k in range(KD):
                    for c in range(KD):
                        last = nc.tensor.transpose(psum[n][:, k * D + c * P:k * D + (c + 1) * P], l1_raw[:, n, c, k * P:(k + 1) * P], ident[:, :])
            last.then_inc(s_l1T, 1)
            pe.wait_ge(s_l1Tc, 2)
            for i, tiles in enumerate(CHUNKS):
                at, n = tiles[0] * P, len(tiles) * P
                pe.wait_ge(s_x3n, i + 1)
                for k in range(KD):
                    for t, tt in enumerate(tiles):
                        last = nc.tensor.transpose(psum[X3_BANK[i] + k][:, t * P:(t + 1) * P], x3n[:, tt * D + k * P:tt * D + (k + 1) * P], ident[:, :])
                    last.then_inc(s_x3T, 1)
                pe.wait_ge(s_x3Tc, 2 * i + 2)
                for c in range(KD):
                    for k in range(KD):
                        last = nc.tensor.matmul(psum[Q_BANK[i] + c][:, 0:n], qg_wT[:, 0, k, c * P:(c + 1) * P], x3T[:, k, at:at + n],
                                                start=(k == 0), stop=(k == KD - 1))
                    last.then_inc(s_q, 1)

            def gate(t):
                for k in range(KD):
                    last = nc.tensor.matmul(psum[4 + t // 2][:, (t % 2) * D:(t % 2 + 1) * D], x3T[:, k, t * P:(t + 1) * P], qg_wT[:, 1, k, :],
                                            start=(k == 0), stop=(k == KD - 1))
                if t % 2:
                    last.then_inc(s_gt, 1)

            def scores(b, n):
                g = b * 16 + n
                lt, hp = n % TB, n // TB
                if not isinstance(g, int) or g >= 2:
                    pe.wait_ge(s_mx, g - 1)
                if n == 0 and (not isinstance(b, int) or b):
                    pe.wait_ge(s_nmc, b)
                for i in range(2):
                    h = 2 * hp + i
                    last = nc.tensor.matmul(psum[n % 2][:, i * S:(i + 1) * S], Qp[0:ROWS_S, h, bass.ds(b * S + lt * P, P)],
                                            Kp[0:ROWS_S, h, bass.ds(b * S, S)], start=True, stop=True)
                last.then_inc(s_S, 1)

            def max_transposes(b):
                pe.wait_ge(s_nm, b + 1)
                pe.sem_inc(s_alone, 1)
                for lt in range(TB):
                    last = nc.tensor.transpose(psbf[0][0:3 * NH, lt * P:(lt + 1) * P], mparts[:, lt, :, :].rearrange("p j h -> p (j h)"), ident_bf[:, :])
                last.then_inc(s_nmp, 1)

            def scores_T(b, hp):
                g = b * 8 + hp
                if not isinstance(g, int) or g >= 2:
                    pe.wait_ge(s_pt, g - 1)
                for i in range(2):
                    h = 2 * hp + i
                    for m in range(TB):
                        last = nc.tensor.matmul(psum[2 + 2 * (hp % 2) + i][:, m * S:(m + 1) * S], Kp[0:ROWS_ST, h, bass.ds(b * S + m * P, P)],
                                                Qp[0:ROWS_ST, h, bass.ds(b * S, S)], start=True, stop=True)
                last.then_inc(s_ST, 1)

            def pv(b, hp):
                g = b * 8 + hp
                c = hp // 2
                pe.wait_ge(s_pt, g + 1)
                if hp == 0:
                    pe.wait_ge(s_vw, b + 1)
                if hp % 2 == 0 and (not isinstance(b, int) or b * 4 + c >= 1):
                    pe.wait_ge(s_A, b * 4 + c)
                for i in range(2):
                    h = 2 * hp + i
                    r = 32 * (h % HC)
                    for m in range(TB):
                        last = nc.tensor.matmul(psum[6][r:r + 32, 0:S], v_wide[:, m, h, :],
                                                probs[hp % 2][:, i, m, :], start=(m == 0), stop=(m == TB - 1))
                last.then_inc(s_PV, 1)

            def gather_sums(b, u):
                pe.wait_ge(s_A, b * 4 + 4)
                if not isinstance(b, int) or b:
                    pe.wait_ge(s_og, b)
                for c in range(NC):
                    last = nc.tensor.matmul(psum[7][0:NH, 0:S], sum_cols[:, c * NH:(c + 1) * NH], attn[u][:, c, :],
                                            start=(c == 0), stop=(c == NC - 1))
                last.then_inc(s_D0, 1)

            def inverse_rows(b, g):
                pe.wait_ge(s_r, b + 1)
                if g:
                    pe.wait_ge(s_an, 2 * b + 1)
                for c in range(2):
                    last = nc.tensor.matmul(psum[7][:, c * S:(c + 1) * S], spread[:, 2 * g + c, :], inv, start=True, stop=True)
                last.then_inc(s_rp, 1)

            def out_product(b, u, lt):
                if lt == 0:
                    pe.wait_ge(s_an, 2 * b + 2)
                for c in range(NC):
                    last = nc.tensor.matmul(psum[7][:, lt * D:(lt + 1) * D], attn[u][:, c, lt * P:(lt + 1) * P], wo_wT[:, c, :],
                                            start=(c == 0), stop=(c == NC - 1))
                if lt == TB - 1:
                    last.then_inc(s_O, 1)

            def map_weights(n):
                if n == 0:
                    pe.wait_ge(s_nmc, B)
                    pe.wait_ge(s_ffw, 32)
                    pe.wait_ge(s_ffb, 32)
                if n >= 2:
                    pe.wait_ge(s_prepc, n - 1)
                for j, src in enumerate(prep_src[n]):
                    last = nc.tensor.transpose(psum[n % 2][:, j * P:(j + 1) * P], src, ident[:, :])
                last.then_inc(s_prep, 1)

            def transpose_x4(t, u, bank=4, at=0):
                pe.wait_ge(s_xf, t + 1)
                pe.sem_inc(s_alone, 1)
                for k in range(KD):
                    last = nc.tensor.transpose(psum[bank][:, at + k * P:at + (k + 1) * P], x4n[u][:, k * P:(k + 1) * P], ident[:, :])
                last.then_inc(s_fT, 1)

            def attention(b, u, ahead=True):
                before = not isinstance(b, int) or b
                for hp in range(8):
                    first, second = UNITS[hp] if ahead else ([], [])
                    if hp == 0:
                        for n in first:
                            scores(b + 1, n)
                        if before:
                            gather_sums(b - 1, 1 - u)
                        for n in second:
                            scores(b + 1, n)
                        pe.wait_ge(s_nmd, 48 * (b + 1))
                    scores_T(b, hp)
                    if before and hp in (2, 3):
                        inverse_rows(b - 1, hp - 2)
                    if hp:
                        pv(b, hp - 1)
                        if before and hp == 4:
                            out_product(b - 1, 1 - u, 0)
                        for n in first:
                            scores(b + 1, n)
                        if before and hp == 4:
                            out_product(b - 1, 1 - u, 1)
                        for n in second:
                            scores(b + 1, n)
                    if ahead and hp == LAST_UNITS + 1:
                        max_transposes(b + 1)
                    if not ahead and hp < len(prep_src) - 2:
                        map_weights(hp)
                if not ahead:
                    for n in range(len(prep_src) - 2, len(prep_src)):
                        map_weights(n)
                    pe.wait_ge(s_prepc, len(prep_src) - 1)
                    transpose_x4(0, 0, 1, 0)
                    transpose_x4(1, 1, 1, D)
                pv(b, 7)

            pe.wait_ge(s_kp, 16 * 9)
            pe.wait_ge(s_qpk[0], 16 * 6)
            for n in range(16):
                scores(0, n)
                if n % 2:
                    if n == 1:
                        pe.wait_ge(s_qp, 4)
                    gate(n // 2)
            max_transposes(0)
            pe.wait_ge(s_qp, 6)
            pe.wait_ge(s_wop, 1)
            for c in range(NC):
                for o in range(KD):
                    last = nc.tensor.transpose(psum[2 + c // 2][:, (c % 2) * D + o * P:(c % 2) * D + (o + 1) * P],
                                               wo_wide[:, o, c * HC:(c + 1) * HC, :].rearrange("p h w -> p (h w)"), ident[:, :])
            last.then_inc(s_l1T, 1)
            pe.wait_ge(s_gtc, 4)
            pe.wait_ge(s_l1Tc, 4)
            pe.wait_ge(s_qpk[1], 16 * 6)
            pe.wait_ge(s_spread, 1)
            attention(0, 0)
            with pe.Fori(1, B - 2, 2) as b:
                attention(b, 1)
                attention(b + 1, 0)
            attention(B - 1, 1, False)
            gather_sums(B - 1, 1)

            def vectors(t, u):
                pe.wait_ge(s_fTc, 2 if isinstance(t, int) and t == 0 else t + 1)
                if isinstance(t, int) and t == 0:
                    pe.wait_ge(s_prepc, len(prep_src))
                elif isinstance(t, int) and t == 1:
                    pe.wait_ge(s_pt, 8 * B)
                else:
                    pe.wait_ge(s_pk, t - 1)
                for h in range(2):
                    part = slice(h * BANK, (h + 1) * BANK)
                    for k in range(KD):
                        nc.tensor.matmul(psum[2 * u + h], x4T[u][:, k, :], aT[:, k, part], start=(k == 0), stop=False)
                        nc.tensor.matmul(psum[2 * u + h], x4T[u][:, k, :], aT_lo[:, k, part], start=False, stop=False)
                pe.wait_ge(s_xlo, t + 1)
                for h in range(2):
                    part = slice(h * BANK, (h + 1) * BANK)
                    for k in range(KD):
                        last = nc.tensor.matmul(psum[2 * u + h], x4T_lo[u][:, k, :], aT[:, k, part], start=False, stop=(k == KD - 1))
                last.then_inc(s_V, 1)

            def transpose_u(t):
                pe.wait_ge(s_u, t + 1)
                for h in range(2):
                    for j in range(4):
                        last = nc.tensor.transpose(psum[4 + h][:, j * P:(j + 1) * P], u_s[:, (4 * h + j) * P:(4 * h + j + 1) * P], ident[:, :])
                    last.then_inc(s_uT, 1)

            def base(t, u):
                if isinstance(t, int) and t == 0:
                    pe.wait_ge(s_A, 4 * B)
                elif isinstance(t, int) and t == 1:
                    pe.wait_ge(s_og, B)
                else:
                    pe.wait_ge(s_fin, t - 1)
                if isinstance(t, int) and t == 0:
                    pe.wait_ge(s_biasr, 1)
                acc = psum[6 + u][:, 0:D]
                for h in range(2):
                    nc.tensor.matmul(acc, ones_part[0:1, :], bias_parts[0:1, h * D:(h + 1) * D], start=(h == 0), stop=False)
                for k in range(KD):
                    nc.tensor.matmul(acc, x4T[u][:, k, :], wT[:, k, :], start=False, stop=False)
                    nc.tensor.matmul(acc, x4T[u][:, k, :], wT_lo[:, k, :], start=False, stop=False)
                    nc.tensor.matmul(acc, x4T_lo[u][:, k, :], wT[:, k, :], start=False, stop=False)

            def delta_high(t, u, h):
                pe.wait_ge(s_uTc, 2 * t + h + 1)
                acc = psum[6 + u][:, 0:D]
                for j in range(4 * h, 4 * h + 4):
                    nc.tensor.matmul(acc, uT[:, j, :], bT[:, j, :], start=False, stop=False)
                    nc.tensor.matmul(acc, uT[:, j, :], bT_lo[:, j, :], start=False, stop=False)

            def delta_low(t, u):
                acc = psum[6 + u][:, 0:D]
                for h in range(2):
                    pe.wait_ge(s_ulo, 2 * t + h + 1)
                    for j in range(4 * h, 4 * h + 4):
                        last = nc.tensor.matmul(acc, uT_lo[:, j, :], bT[:, j, :], start=False, stop=(j == JA - 1))
                last.then_inc(s_D, 1)

            def maps(t, u, ahead=3):
                if ahead >= 2:
                    vectors(t + 2, u)
                transpose_u(t)
                if ahead >= 1:
                    base(t + 1, 1 - u)
                delta_high(t, u, 0)
                if ahead >= 3:
                    pe.wait_ge(s_uTw, 2 * t + 1)
                    transpose_x4(t + 3, 1 - u)
                delta_high(t, u, 1)
                delta_low(t, u)

            vectors(0, 0)
            inverse_rows(B - 1, 0)
            base(0, 0)
            inverse_rows(B - 1, 1)
            for lt in range(TB):
                out_product(B - 1, 1, lt)
            vectors(1, 1)
            transpose_x4(2, 0)
            maps(0, 0)
            maps(1, 1)
            with pe.Fori(2, T - 4, 2) as t:
                maps(t, 0)
                maps(t + 1, 1)
            maps(T - 4, 0)
            maps(T - 3, 1, 2)
            maps(T - 2, 0, 1)
            maps(T - 1, 1, 0)


_INS = ["x", "ctx_2048", "mask_BxS2_bk0", "g_xattn", "g_ffn", "L0_ffn_gate_w", "L0_ffn_w1", "L0_ffn_w2", "L0_ffn_w3",
        "L1_xattn_norm_w", "L1_xattn_wq", "L1_xattn_wk", "L1_xattn_wv", "L1_xattn_wo", "L1_xattn_wg",
        "L1_ffn_A", "L1_ffn_B", "L1_ffn_W", "L1_ffn_bias"]


def kernel(**inputs):
    import numpy as _np
    import concourse.bacc as _bacc
    from concourse import mybir as _mybir
    from concourse.bass_utils import run_bass_kernel_spmd as _run

    nc = _bacc.Bacc("TRN2", target_bir_lowering=False, num_devices=1)
    arrays, aps = {}, {}
    for name in _INS:
        x = _np.ascontiguousarray(inputs[name])
        arrays[f"in_{name}_dram"] = x
        aps[name] = nc.dram_tensor(f"in_{name}_dram", x.shape, _mybir.dt.from_np(x.dtype), kind="ExternalInput").ap()
    aps["out"] = nc.dram_tensor("out_dram", (B, S, D), _mybir.dt.float32, kind="ExternalOutput").ap()
    flamingo(nc, aps)
    r = _run(nc, [arrays], core_ids=[0])
    return r.results[0]["out_dram"]
```
